# Optimizing a Trainium2 kernel written in Bass

```python
import numpy as np
import jax
import jax.numpy as jnp

def _softmax(x, axis=-1):
    return jax.nn.softmax(x, axis=axis)

def _gelu(x):
    return jax.nn.gelu(x, approximate=True)

def _silu(x):
    return jax.nn.silu(x)

def _sigmoid(x):
    return jax.nn.sigmoid(x)

def _layernorm(x, axis=-1, eps=1e-05):
    m = jnp.mean(x, axis=axis, keepdims=True)
    v = jnp.var(x, axis=axis, keepdims=True)
    return (x - m) / jnp.sqrt(v + eps)

def _scatter_add(tgt, idx, src, axis=0):
    return tgt.at[idx].add(src)

def _segment_sum(src, seg, n):
    return jax.ops.segment_sum(src, seg, n)
kernel_name = 'mk_hybrid_d1_jaxref_r8_614759'

def setup_inputs(seed: int=0):
    np.random.seed(seed)
    _w = jnp.asarray

    def _L0_attn_a_setup():
        import jax, jax.numpy as jnp
        import numpy as np
        HEAD_NUM = 16
        key = jax.random.key(seed)
        ks = jax.random.split(key, 9)
        B, S, D = (4, 256, 128)

        def xavier(k, shape):
            limit = jnp.sqrt(6.0 / (shape[0] + shape[1]))
            return jax.random.uniform(k, shape, jnp.float32, -limit, limit)
        return {'x': jax.random.normal(ks[0], (B, S, D), jnp.float32), 'Wq': xavier(ks[1], (D, D)), 'bq': jnp.zeros((D,), jnp.float32), 'Wk': xavier(ks[2], (D, D)), 'bk': jnp.zeros((D,), jnp.float32), 'Wv': xavier(ks[3], (D, D)), 'bv': jnp.zeros((D,), jnp.float32), 'Wo': xavier(ks[4], (D, D)), 'bo': jnp.zeros((D,), jnp.float32)}
    _L0_attn_a_in = _L0_attn_a_setup()

    def _L0_attn_b_setup():
        import jax, jax.numpy as jnp
        import numpy as np
        B, S, DIM = (2, 256, 128)
        H, W = (16, 32)
        HD = DIM // H
        SCALE = HD ** (-0.5)
        key = jax.random.key(seed)
        ks = jax.random.split(key, 9)
        std = DIM ** (-0.5)
        return {'x': jax.random.normal(ks[0], (B, S, DIM), dtype=jnp.float32), 'Wq': jax.random.normal(ks[1], (DIM, DIM), dtype=jnp.float32) * std, 'bq': jnp.zeros((DIM,), dtype=jnp.float32), 'Wk': jax.random.normal(ks[2], (DIM, DIM), dtype=jnp.float32) * std, 'bk': jnp.zeros((DIM,), dtype=jnp.float32), 'Wv': jax.random.normal(ks[3], (DIM, DIM), dtype=jnp.float32) * std, 'bv': jnp.zeros((DIM,), dtype=jnp.float32), 'Wo': jax.random.normal(ks[4], (DIM, DIM), dtype=jnp.float32) * std, 'bo': jnp.zeros((DIM,), dtype=jnp.float32)}
    _L0_attn_b_in = _L0_attn_b_setup()

    def _L0_ffn_setup():
        import jax, jax.numpy as jnp
        import numpy as np
        from jax import lax
        HIDDEN = 128
        INTER = 64
        E = 64
        K = 6
        G = 8
        TG = 4
        NSH = 2
        ISH = INTER * NSH

        def _moe_forward(hidden_states, gate_w, gate_bias, eg_w, eu_w, ed_w, sg_w, su_w, sd_w):
            B, S, H = hidden_states.shape
            x = hidden_states.reshape(-1, H)
            T = x.shape[0]
            shared = jax.nn.silu(x @ sg_w.T) * (x @ su_w.T) @ sd_w.T
            logits = x @ gate_w.T
            scores = jax.nn.sigmoid(logits) + gate_bias
            group_scores = scores.reshape(T, G, E // G).max(axis=-1)
            _, sel_groups = lax.top_k(group_scores, TG)
            group_mask = jnp.zeros((T, G), scores.dtype).at[jnp.arange(T)[:, None], sel_groups].set(1.0)
            mask = jnp.repeat(group_mask, E // G, axis=1)
            masked_scores = scores * mask
            topk_w, topk_i = lax.top_k(masked_scores, K)
            topk_w = topk_w / (topk_w.sum(axis=-1, keepdims=True) + 1e-08)
            comb = jnp.zeros((T, E), x.dtype).at[jnp.arange(T)[:, None], topk_i].add(topk_w)
            h = jax.nn.silu(jnp.einsum('th,eih->eti', x, eg_w)) * jnp.einsum('th,eih->eti', x, eu_w)
            routed = jnp.einsum('eti,ehi,te->th', h, ed_w, comb)
            return (shared + routed).reshape(B, S, H)
        key = jax.random.key(seed)
        ks = jax.random.split(key, 9)
        s = 0.02
        return {'hidden_states': jax.random.normal(ks[0], (1, 128, HIDDEN), jnp.float32), 'gate_w': jax.random.normal(ks[1], (E, HIDDEN), jnp.float32) * s, 'gate_bias': jnp.zeros((E,), jnp.float32), 'eg_w': jax.random.normal(ks[2], (E, INTER, HIDDEN), jnp.float32) * s, 'eu_w': jax.random.normal(ks[3], (E, INTER, HIDDEN), jnp.float32) * s, 'ed_w': jax.random.normal(ks[4], (E, HIDDEN, INTER), jnp.float32) * s, 'sg_w': jax.random.normal(ks[5], (ISH, HIDDEN), jnp.float32) * s, 'su_w': jax.random.normal(ks[6], (ISH, HIDDEN), jnp.float32) * s, 'sd_w': jax.random.normal(ks[7], (HIDDEN, ISH), jnp.float32) * s}
    _L0_ffn_in = _L0_ffn_setup()
    _d = {'L0_attn_a_x': _L0_attn_a_in['x'], 'L0_attn_a_Wq': _L0_attn_a_in['Wq'], 'L0_attn_a_bq': _L0_attn_a_in['bq'], 'L0_attn_a_Wk': _L0_attn_a_in['Wk'], 'L0_attn_a_bk': _L0_attn_a_in['bk'], 'L0_attn_a_Wv': _L0_attn_a_in['Wv'], 'L0_attn_a_bv': _L0_attn_a_in['bv'], 'L0_attn_a_Wo': _L0_attn_a_in['Wo'], 'L0_attn_a_bo': _L0_attn_a_in['bo'], 'L0_attn_b_Wq': _L0_attn_b_in['Wq'], 'L0_attn_b_bq': _L0_attn_b_in['bq'], 'L0_attn_b_Wk': _L0_attn_b_in['Wk'], 'L0_attn_b_bk': _L0_attn_b_in['bk'], 'L0_attn_b_Wv': _L0_attn_b_in['Wv'], 'L0_attn_b_bv': _L0_attn_b_in['bv'], 'L0_attn_b_Wo': _L0_attn_b_in['Wo'], 'L0_attn_b_bo': _L0_attn_b_in['bo'], 'L0_ffn_gate_w': _L0_ffn_in['gate_w'], 'L0_ffn_gate_bias': _L0_ffn_in['gate_bias'], 'L0_ffn_eg_w': _L0_ffn_in['eg_w'], 'L0_ffn_eu_w': _L0_ffn_in['eu_w'], 'L0_ffn_ed_w': _L0_ffn_in['ed_w'], 'L0_ffn_sg_w': _L0_ffn_in['sg_w'], 'L0_ffn_su_w': _L0_ffn_in['su_w'], 'L0_ffn_sd_w': _L0_ffn_in['sd_w']}
    _x0 = _d['L0_attn_a_x']
    _d['L0_attn_a_x'] = jax.random.normal(jax.random.fold_in(jax.random.key(seed), 1), (2, 1024, 128), dtype=_x0.dtype)
    del _x0
    return _d

def reference(L0_attn_a_x, L0_attn_a_Wq, L0_attn_a_bq, L0_attn_a_Wk, L0_attn_a_bk, L0_attn_a_Wv, L0_attn_a_bv, L0_attn_a_Wo, L0_attn_a_bo, L0_attn_b_Wq, L0_attn_b_bq, L0_attn_b_Wk, L0_attn_b_bk, L0_attn_b_Wv, L0_attn_b_bv, L0_attn_b_Wo, L0_attn_b_bo, L0_ffn_gate_w, L0_ffn_gate_bias, L0_ffn_eg_w, L0_ffn_eu_w, L0_ffn_ed_w, L0_ffn_sg_w, L0_ffn_su_w, L0_ffn_sd_w):

    def _L0_attn_a_ref(x, Wq, bq, Wk, bk, Wv, bv, Wo, bo):
        import jax, jax.numpy as jnp
        import numpy as np
        HEAD_NUM = 16
        B, S, D = x.shape
        H = HEAD_NUM
        hd = D // H

        def proj(W, b):
            return (x @ W.T + b).reshape(B, S, H, hd).transpose(0, 2, 1, 3)
        Q, K, V = (proj(Wq, bq), proj(Wk, bk), proj(Wv, bv))
        scale = 1.0 / jnp.sqrt(jnp.float32(hd))
        scores = jnp.einsum('bhqd,bhkd->bhqk', Q, K) * scale
        attn = jax.nn.softmax(scores, axis=-1)
        out = jnp.einsum('bhqk,bhkd->bhqd', attn, V)
        out = out.transpose(0, 2, 1, 3).reshape(B, S, D)
        return out @ Wo.T + bo

    def _L0_attn_b_ref(x, Wq, bq, Wk, bk, Wv, bv, Wo, bo):
        import jax, jax.numpy as jnp
        import numpy as np
        B, S, DIM = (2, 256, 128)
        H, W = (16, 32)
        HD = DIM // H
        SCALE = HD ** (-0.5)
        b, s, dim = x.shape
        q = (x @ Wq + bq).reshape(b, s, H, HD).transpose(0, 2, 1, 3)
        k = (x @ Wk + bk).reshape(b, s, H, HD).transpose(0, 2, 1, 3)
        v = (x @ Wv + bv).reshape(b, s, H, HD).transpose(0, 2, 1, 3)
        scores = jnp.einsum('bhid,bhjd->bhij', q, k) * SCALE
        i = jnp.arange(s)[:, None]
        j = jnp.arange(s)[None, :]
        valid = (j <= i) & (j >= i - W + 1)
        scores = jnp.where(valid, scores, -jnp.inf)
        attn = jax.nn.softmax(scores, axis=-1)
        out = jnp.einsum('bhij,bhjd->bhid', attn, v)
        out = out.transpose(0, 2, 1, 3).reshape(b, s, dim)
        return out @ Wo + bo

    def _L0_ffn_ref(hidden_states, gate_w, gate_bias, eg_w, eu_w, ed_w, sg_w, su_w, sd_w):
        import jax, jax.numpy as jnp
        import numpy as np
        from jax import lax
        HIDDEN = 128
        INTER = 64
        E = 64
        K = 6
        G = 8
        TG = 4
        NSH = 2
        ISH = INTER * NSH

        def _moe_forward(hidden_states, gate_w, gate_bias, eg_w, eu_w, ed_w, sg_w, su_w, sd_w):
            B, S, H = hidden_states.shape
            x = hidden_states.reshape(-1, H)
            T = x.shape[0]
            shared = jax.nn.silu(x @ sg_w.T) * (x @ su_w.T) @ sd_w.T
            logits = x @ gate_w.T
            scores = jax.nn.sigmoid(logits) + gate_bias
            group_scores = scores.reshape(T, G, E // G).max(axis=-1)
            _, sel_groups = lax.top_k(group_scores, TG)
            group_mask = jnp.zeros((T, G), scores.dtype).at[jnp.arange(T)[:, None], sel_groups].set(1.0)
            mask = jnp.repeat(group_mask, E // G, axis=1)
            masked_scores = scores * mask
            topk_w, topk_i = lax.top_k(masked_scores, K)
            topk_w = topk_w / (topk_w.sum(axis=-1, keepdims=True) + 1e-08)
            comb = jnp.zeros((T, E), x.dtype).at[jnp.arange(T)[:, None], topk_i].add(topk_w)
            h = jax.nn.silu(jnp.einsum('th,eih->eti', x, eg_w)) * jnp.einsum('th,eih->eti', x, eu_w)
            routed = jnp.einsum('eti,ehi,te->th', h, ed_w, comb)
            return (shared + routed).reshape(B, S, H)
        return _moe_forward(hidden_states, gate_w, gate_bias, eg_w, eu_w, ed_w, sg_w, su_w, sd_w)
    x = L0_attn_a_x
    x = x + _L0_attn_a_ref(_layernorm(x, axis=-1), L0_attn_a_Wq, L0_attn_a_bq, L0_attn_a_Wk, L0_attn_a_bk, L0_attn_a_Wv, L0_attn_a_bv, L0_attn_a_Wo, L0_attn_a_bo)
    x = x + _L0_ffn_ref(_layernorm(x, axis=-1), L0_ffn_gate_w, L0_ffn_gate_bias, L0_ffn_eg_w, L0_ffn_eu_w, L0_ffn_ed_w, L0_ffn_sg_w, L0_ffn_su_w, L0_ffn_sd_w)
    x = x + _L0_attn_b_ref(_layernorm(x, axis=-1), L0_attn_b_Wq, L0_attn_b_bq, L0_attn_b_Wk, L0_attn_b_bk, L0_attn_b_Wv, L0_attn_b_bv, L0_attn_b_Wo, L0_attn_b_bo)
    x = x + _L0_ffn_ref(_layernorm(x, axis=-1), L0_ffn_gate_w, L0_ffn_gate_bias, L0_ffn_eg_w, L0_ffn_eu_w, L0_ffn_ed_w, L0_ffn_sg_w, L0_ffn_su_w, L0_ffn_sd_w)
    return x

_drawn_inputs = setup_inputs


def setup_inputs(seed=0):
    import zlib

    import numpy as np

    out = dict(_drawn_inputs(seed))
    spreads = {'L0_attn_a_bq': (0.0, 0.658),
     'L0_attn_a_bk': (0.0, 0.8),
     'L0_attn_a_bv': (0.0, 0.1),
     'L0_attn_a_bo': (0.0, 0.1),
     'L0_attn_b_bq': (0.0, 0.338),
     'L0_attn_b_bk': (0.0, 0.8),
     'L0_attn_b_bv': (0.0, 0.1),
     'L0_attn_b_bo': (0.0, 0.1),
     'L0_ffn_gate_bias': (0.0, 0.8)}
    factors = {'L0_ffn_gate_w': 8.0,
     'L0_ffn_eg_w': 8.0,
     'L0_ffn_eu_w': 8.0,
     'L0_ffn_ed_w': 8.0,
     'L0_ffn_sg_w': 5.27,
     'L0_ffn_su_w': 5.257,
     'L0_ffn_sd_w': 5.229}
    for name, (base, spread) in spreads.items():
        noise = np.random.default_rng([zlib.crc32(name.encode()), seed]).standard_normal(out[name].shape)
        drawn = base * np.exp(spread * noise) if base else spread * noise
        out[name] = jnp.asarray(drawn.astype(out[name].dtype))
    for name, factor in factors.items():
        out[name] = (out[name] * factor).astype(out[name].dtype)
    return out
```

```python
from contextlib import ExitStack

import concourse.bass as bass
from concourse import mybir

F32 = mybir.dt.float32
BF16 = mybir.dt.bfloat16
F16 = mybir.dt.float16
I32 = mybir.dt.int32
U32 = mybir.dt.uint32
ACT = mybir.ActivationFunctionType
ALU = mybir.AluOpType
AX = mybir.AxisListType

P = 128
B, S, C = 2, 1024, 128
NT = B * S // P
TB = S // P
H, HD = 16, 8
HG = 4
G = H // HG
NG = B * G
CH = 512
NC = B * S // CH
SLOTS = 6
QSLOT = {0: (0, 3, 5), 1: (1, 4), 2: (2,)}
KSLOT = {0: (0, 1, 2), 1: (3, 4), 2: (5,)}
SR = SLOTS * HD
MAXROW = 64
VW = 32
WIN = 32
BAND = P + WIN
BARRED = -1e30
EPS = 1e-5
SCALE = float(HD) ** -0.5


class Env:
    pass


def layer_norm_and_transpose(nc, env, tag, finish):
    with ExitStack() as ctx:
        sb = lambda n, s, d: ctx.enter_context(nc.sbuf_tensor(f"{tag}_{n}", s, d))
        sem = lambda n: ctx.enter_context(nc.semaphore(f"{tag}_{n}"))
        stats = sb("stats", [P, NT, 6], F32)
        mv = sb("mv", [P, NT, 2], F32)
        ve = sb("ve", [P, NT], F32)
        sd = sb("sd", [P, NT], F32)
        r0 = sb("r0", [P, NT], F32)
        r1 = sb("r1", [P, NT], F32)
        rstd = sb("rstd", [P, NT], F32)
        nmr = sb("nmr", [P, NT], F32)
        xn = sb("xn", [P, NT, C], F32)
        tp = [ctx.enter_context(nc.psum_tensor(f"{tag}_tp{i}", [P, CH], F32)) for i in range(2)]
        dve_step, var_ready, sd_ready, xn_ready, turned, copied = map(
            sem, ("dve_step", "var_ready", "sd_ready", "xn_ready", "turned", "copied"))
        block = ctx.enter_context(nc.Block())

        @block.vector
        def _(dve):
            for t in range(NT):
                dve.bn_stats(stats[:, t, :], env.x[:, t, :]).then_inc(dve_step, 1)
            dve.wait_ge(dve_step, NT)
            for t in range(NT):
                dve.bn_aggr(mv[:, t, :], stats[:, t, :]).then_inc(dve_step, 1)
            dve.wait_ge(dve_step, 2 * NT)
            dve.tensor_scalar(ve[:, :], mv[:, :, 1], EPS, None, ALU.add).then_inc(var_ready, 1)
            dve.wait_ge(sd_ready, 1)
            dve.reciprocal(r0[:, :], sd[:, :]).then_inc(dve_step, 1)
            dve.wait_ge(dve_step, 2 * NT + 1)
            dve.tensor_tensor(r1[:, :], r0[:, :], r0[:, :], ALU.mult).then_inc(dve_step, 1)
            dve.wait_ge(dve_step, 2 * NT + 2)
            dve.scalar_tensor_tensor(r1[:, :], r1[:, :], -0.5, ve[:, :], ALU.mult, ALU.mult).then_inc(dve_step, 1)
            dve.wait_ge(dve_step, 2 * NT + 3)
            dve.scalar_tensor_tensor(rstd[:, :], r1[:, :], 1.5, r0[:, :], ALU.add, ALU.mult).then_inc(dve_step, 1)
            dve.wait_ge(dve_step, 2 * NT + 4)
            dve.scalar_tensor_tensor(nmr[:, :], mv[:, :, 0], -1.0, rstd[:, :], ALU.mult, ALU.mult).then_inc(dve_step, 1)
            dve.wait_ge(dve_step, 2 * NT + 5)
            for t in range(NT):
                dve.tensor_scalar(xn[:, t, :], env.x[:, t, :], mv[:, t, 0:1], rstd[:, t:t + 1],
                                  ALU.subtract, ALU.mult).then_inc(xn_ready, 1)

        @block.tensor
        def _(pe):
            for t in range(NT):
                c = t // 4
                if c >= 2 and t % 4 == 0:
                    pe.wait_ge(copied, c - 1)
                pe.wait_ge(xn_ready, t + 1)
                pe.transpose(tp[c % 2][:, (t % 4) * P:(t % 4 + 1) * P], xn[:, t, :], env.ident[:, :]).then_inc(turned, 1)

        @block.scalar
        def _(act):
            act.wait_ge(var_ready, 1)
            act.activation(sd[:, :], ve[:, :], ACT.Sqrt).then_inc(sd_ready, 1)
            for c in range(NC):
                act.wait_ge(turned, 4 * (c + 1))
                finish(act, c, tp[c % 2]).then_inc(copied, 1)


def project_qkv(nc, env, tag):
    with ExitStack() as ctx:
        sb = lambda n, s, d: ctx.enter_context(nc.sbuf_tensor(f"{tag}_{n}", s, d))
        sem = lambda n: ctx.enter_context(nc.semaphore(f"{tag}_{n}"))
        full = sb("full", [P, 2, CH], F32)
        rest = sb("rest", [P, 2, CH], F32)
        part = sb("part", [P, 2, 3, B * S], BF16)
        pq = [ctx.enter_context(nc.psum_tensor(f"{tag}_pq{i}", [P, CH], F32)) for i in range(4)]
        pv = [ctx.enter_context(nc.psum_tensor(f"{tag}_pv{i}", [P, CH], F32)) for i in range(2)]
        mm_done, v_done, full_ready, high_ready, rest_ready, mid_ready, low_ready, v_out, stored = map(sem, (
            "mm_done", "v_done", "full_ready", "high_ready", "rest_ready", "mid_ready", "low_ready", "v_out", "stored"))
        block = ctx.enter_context(nc.Block())
        NQ = 2 * NC

        @block.tensor
        def _(pe):
            for n in range(NQ):
                w, c = n // NC, n % NC
                if n >= 4:
                    pe.wait_ge(full_ready, n - 3)
                pe.matmul(pq[n % 4][:, :], env.wqk[:, w, :], env.xnT[:, c * CH:(c + 1) * CH],
                          start=True, stop=True).then_inc(mm_done, 1)
            for t in range(NT):
                if t >= 8 and t % 4 == 0:
                    pe.wait_ge(v_out, t // 4 - 1)
                pe.matmul(pv[t // 4 % 2][:, (t % 4) * P:(t % 4 + 1) * P], env.xnT[:, t * P:(t + 1) * P],
                          env.wv[:, :], start=True, stop=True).then_inc(v_done, 1)

        @block.scalar
        def _(act):
            for n in range(NQ):
                w, c = n // NC, n % NC
                act.wait_ge(mm_done, n + 1)
                if n >= 2:
                    act.wait_ge(low_ready, n - 1)
                act.activation(full[:, n % 2, :], pq[n % 4][:, :], ACT.Identity,
                               bias=env.bqk[:, w:w + 1]).then_inc(full_ready, 1)
                act.wait_ge(full_ready, n + 1)
                act.copy(part[:, w, 0, c * CH:(c + 1) * CH], full[:, n % 2, :]).then_inc(high_ready, 1)

        @block.vector
        def _(dve):
            for n in range(NQ):
                w, c = n // NC, n % NC
                cs = slice(c * CH, (c + 1) * CH)
                dve.wait_ge(high_ready, n + 1)
                dve.tensor_tensor(rest[:, n % 2, :], full[:, n % 2, :], part[:, w, 0, cs], ALU.subtract).then_inc(rest_ready, 1)
                dve.wait_ge(rest_ready, n + 1)
                dve.tensor_copy(part[:, w, 1, cs], rest[:, n % 2, :]).then_inc(mid_ready, 1)
                dve.wait_ge(mid_ready, n + 1)
                dve.tensor_tensor(part[:, w, 2, cs], rest[:, n % 2, :], part[:, w, 1, cs], ALU.subtract).then_inc(low_ready, 1)
            for c in range(NC):
                dve.wait_ge(v_done, 4 * (c + 1))
                bias = env.bv[:, :].rearrange("p (a g c) -> p a g c", a=1, g=G).to_broadcast([P, 4, G, HG * HD])
                b, k = c // 2, c % 2
                dve.tensor_tensor(env.vn[:, G * b:G * b + G, 4 * k:4 * k + 4, :].rearrange("p g a c -> p a g c"),
                                  pv[c % 2][:, :].rearrange("p (a g c) -> p a g c", a=4, g=G),
                                  bias, ALU.add).then_inc(v_out, 1)

        def store(eng, w):
            for part_no, slots in (QSLOT, KSLOT)[w].items():
                eng.wait_ge((high_ready, mid_ready, low_ready)[part_no], NC * (w + 1))
                for r in slots:
                    for g in range(G):
                        eng.dma_start(env.stack[w, :, g, r].rearrange("b d j t -> (d j) b t"),
                                      part[32 * g:32 * g + 32, w, part_no, :].rearrange("p (b t) -> p b t", b=B)
                                      ).then_inc(stored, 16)

        @block.sync
        def _(sp):
            store(sp, 0)
            store(sp, 1)
            sp.wait_ge(stored, 16 * 2 * SLOTS * G)


def attend_full(nc, env, tag):
    STEPS = 2 * TB
    FREE = 2
    AHEAD = 4
    NS = 4 * STEPS
    with ExitStack() as ctx:
        sb = lambda n, s, d: ctx.enter_context(nc.sbuf_tensor(f"{tag}_{n}", s, d))
        ps = lambda n, s, d: ctx.enter_context(nc.psum_tensor(f"{tag}_{n}", s, d))
        sem = lambda n: ctx.enter_context(nc.semaphore(f"{tag}_{n}"))
        qs = [sb(f"qs{i}", [P, HG, S], BF16) for i in range(3)]
        ks = [sb(f"ks{i}", [P, HG, S], BF16) for i in range(3)]
        vg = [sb(f"vg{i}", [P, TB, HG, VW], F32) for i in range(3)]
        prob = [sb(f"prob{i}", [P, 2, CH], F32) for i in range(4)]
        mx = [sb(f"mx{i}", [P, HG * TB, 2], F32) for i in range(3)]
        m1 = sb("m1", [P, HG * TB], F32)
        m2 = sb("m2", [P, HG * TB], F32)
        mparts = sb("mparts", [P, 3, HG * TB], BF16)
        mt = sb("mt", [3 * HG * TB, P], BF16)
        sc = [ps(f"sc{i}", [P, CH], F32) for i in range(2)]
        st = [ps(f"st{i}", [P, 2, CH], F32) for i in range(2)]
        pv = ps("pv", [P, CH], F32)
        turn = ps("turn", [P, 2 * CH], BF16)
        loaded = [sem(f"loaded{i}") for i in range(3)]
        (q_init, v_init, cleared, v_ready, sc_done, red_done, m_step, turned, m_copied, max_ready,
         st_done, exp_done, pv_done, u_out) = map(sem, (
            "q_init", "v_init", "cleared", "v_ready", "sc_done", "red_done", "m_step", "turned", "m_copied",
            "max_ready", "st_done", "exp_done", "pv_done", "u_out"))
        block = ctx.enter_context(nc.Block())

        Q_INIT = 4 * 3
        LOOPED = 6

        def stages(eng, stage):
            with eng.Fori(0, LOOPED // 3) as i:
                for k in range(3):
                    stage(i, k, True, True)
            stage(LOOPED // 3, 0, True, False)
            stage(LOOPED // 3, 1, False, False)

        def score_blocks(s, k, nxt, nxt2):
            if s < STEPS - AHEAD:
                return [(1, (k + 1) % 3, s + AHEAD)] if nxt else []
            return [(2, (k + 2) % 3, s - (STEPS - AHEAD))] if nxt2 else []

        @block.sync
        def _(sp):
            def load(n, k):
                for t, w in ((qs[k], 0), (ks[k], 1)):
                    sp.dma_start(t[0:SR, :, :].rearrange("p j t -> p (j t)"),
                                 env.stackn[w, n, :, :]).then_inc(loaded[k], 16)

            def max_rows(n, k):
                sp.wait_ge(m_copied, n + 1)
                sp.sem_inc(env.sp_passed, 1)
                for i in range(3):
                    sp.dma_start(qs[k][MAXROW + i:MAXROW + i + 1, :, :].rearrange("p j t -> p (j t)"),
                                 mt[HG * TB * i:HG * TB * (i + 1), :]).then_inc(max_ready, 16)

            sp.wait_ge(q_init, Q_INIT)
            for n in range(2):
                load(n, n)
            max_rows(0, 0)

            def stage(r, k, nxt, nxt2):
                n = r * 3 + k
                if nxt2:
                    sp.wait_ge(st_done, n * 2 * STEPS)
                    sp.sem_inc(env.sp_passed, 1)
                    load(n + 2, (k + 2) % 3)
                if nxt:
                    max_rows(n + 1, (k + 1) % 3)
            stages(sp, stage)

        @block.gpsimd
        def _(pool):
            for k in range(3):
                pool.memset(ks[k][MAXROW:P, :, :], 1.0).then_inc(q_init, 1)
            pool.drain()
            for k in range(3):
                pool.memset(vg[k][:, :, :, :], 1.0).then_inc(v_init, 1)

            def copy_v(n, k):
                pool.tensor_copy(vg[k][:, :, :, 0:HD],
                                 env.vn[:, bass.ds(n, 1), :, :].rearrange("p o t (j d) -> p (o t) j d", j=HG)
                                 ).then_inc(v_ready, 1)

            pool.wait_ge(v_init, 3)
            copy_v(0, 0)
            pool.wait_ge(q_init, Q_INIT)

            def stage(r, k, nxt, nxt2):
                n = r * 3 + k
                if nxt2:
                    pool.wait_ge(st_done, n * 2 * STEPS)
                    pool.wait_ge(v_ready, n + 1)
                    pool.sem_inc(env.pool_passed, 1)
                    pool.memset(qs[(k + 2) % 3][MAXROW:MAXROW + 3, :, :].bitcast(U32), 0).then_inc(cleared, 1)
                    pool.wait_ge(cleared, n + 1)
                if nxt:
                    pool.wait_ge(pv_done, n * STEPS)
                    pool.sem_inc(env.pool_passed, 1)
                    copy_v(n + 1, (k + 1) % 3)
            stages(pool, stage)

        @block.tensor
        def _(pe):
            def scores(n, k, blk, half):
                i0 = 4 * blk + 2 * half
                j, qt = i0 // 2 // TB, i0 // 2 % TB
                for h in range(2):
                    i = i0 + h
                    pe.wait_ge(red_done, n * NS + i + 1)
                    pe.matmul(sc[i % 2][:, :], qs[k][:, j, qt * P:(qt + 1) * P], ks[k][:, j, h * CH:(h + 1) * CH],
                              start=True, stop=True).then_inc(sc_done, 1)

            def weigh(n, k, s):
                qh, kc = s // TB, s % TB
                pe.wait_ge(exp_done, FREE + n * 2 * STEPS + 2 * s + 2)
                if kc == 0:
                    pe.wait_ge(u_out, n * 2 + qh)
                for j in range(HG):
                    mm = pe.matmul(pv[32 * j:32 * j + 32, :], vg[k][:, kc, j, :],
                                   prob[(2 * s + j // 2) % 4][:, j % 2, :], start=kc == 0, stop=kc == TB - 1)
                mm.then_inc(pv_done, 1)

            def turn_max(n):
                pe.wait_ge(m_step, 5 * n + 5)
                pe.transpose(turn[0:3 * HG * TB, 0:P], mparts[:, :, :].rearrange("p a m -> p (a m)"),
                             env.ident16[:, :]).then_inc(turned, 1)

            for n in range(2):
                pe.wait_ge(loaded[n], 32)
                pe.wait_ge(q_init, Q_INIT)
                for blk in range(STEPS if n == 0 else AHEAD):
                    scores(n, n, blk, 0)
                    scores(n, n, blk, 1)
                if n == 0:
                    turn_max(0)

            def stage(r, k, nxt, nxt2):
                n = r * 3 + k
                pe.wait_ge(max_ready, 48 * n + 48)
                pe.wait_ge(v_ready, n + 1)
                for s in range(STEPS):
                    qh, kc = s // TB, s % TB
                    blocks = score_blocks(s, k, nxt, nxt2)
                    if s == STEPS - AHEAD and nxt2:
                        pe.wait_ge(loaded[(k + 2) % 3], (r + (k + 2) // 3) * 32 + 32)
                        pe.wait_ge(cleared, n + 1)
                    for pr in range(2):
                        e = 2 * s + pr
                        pe.wait_ge(exp_done, n * 2 * STEPS + e + 1)
                        for h in range(2):
                            j = 2 * pr + h
                            mm = pe.matmul(st[pr][:, h, :], ks[k][:, j, kc * P:(kc + 1) * P],
                                           qs[k][:, j, qh * CH:(qh + 1) * CH], start=True, stop=True)
                        mm.then_inc(st_done, 1)
                        for off, kk, blk in blocks:
                            scores(n + off, kk, blk, pr)
                    if s:
                        weigh(n, k, s - 1)
                    if s == STEPS - AHEAD + 1 and nxt:
                        turn_max(n + 1)
                weigh(n, k, STEPS - 1)
            stages(pe, stage)

        @block.scalar
        def _(act):
            act.sem_inc(exp_done, FREE)

            def copy_max(n):
                act.wait_ge(turned, n + 1)
                if not (isinstance(n, int) and n == 0):
                    act.wait_ge(max_ready, n * 48)
                act.copy(mt[:, :], turn[0:3 * HG * TB, 0:P]).then_inc(m_copied, 1)

            copy_max(0)

            def stage(r, k, nxt, nxt2):
                n = r * 3 + k
                for s in range(STEPS):
                    qh = s // TB
                    if s >= 2:
                        act.wait_ge(pv_done, n * STEPS + s - 1)
                    for pr in range(2):
                        e = 2 * s + pr
                        act.wait_ge(st_done, n * 2 * STEPS + e + 1)
                        act.activation(prob[e % 4][:, :, :].rearrange("p a c -> p (a c)"),
                                       st[pr][:, :, :].rearrange("p a c -> p (a c)"), ACT.Exp,
                                       scale=SCALE).then_inc(exp_done, 1)
                    if s in (TB, STEPS - 1):
                        half = 0 if s == TB else 1
                        act.wait_ge(pv_done, n * STEPS + TB * (half + 1))
                        act.copy(env.u[:, bass.ds(n, 1), half * CH:(half + 1) * CH].rearrange("p o c -> p (o c)"),
                                 pv[:, :]).then_inc(u_out, 1)
                    if s == STEPS - AHEAD + 1 and nxt:
                        copy_max(n + 1)
            stages(act, stage)

        @block.vector
        def _(dve):
            for k in range(3):
                for a, b in ((32, 64), (64, P)):
                    dve.memset(qs[k][a:b, :, :].bitcast(U32), 0).then_inc(q_init, 1)
                dve.memset(ks[k][32:MAXROW, :, :].bitcast(U32), 0).then_inc(q_init, 1)
            dve.sem_inc(red_done, FREE)

            def reduce_block(n, k, blk):
                for i in range(4 * blk, 4 * blk + 4):
                    dve.wait_ge(sc_done, n * NS + i + 1)
                    dve.tensor_reduce(mx[k][:, i // 2, i % 2:i % 2 + 1], sc[i % 2][:, :], AX.X, ALU.max).then_inc(red_done, 1)

            def cut_max(n, k):
                dve.wait_ge(red_done, FREE + (n + 1) * NS)
                dve.tensor_reduce(m1[:, :], mx[k][:, :, :], AX.X, ALU.max, negate=True).then_inc(m_step, 1)
                if not (isinstance(n, int) and n == 0):
                    dve.wait_ge(turned, n)
                dve.wait_ge(m_step, 5 * n + 1)
                dve.tensor_copy(mparts[:, 0, :], m1[:, :]).then_inc(m_step, 1)
                dve.wait_ge(m_step, 5 * n + 2)
                dve.tensor_tensor(m2[:, :], m1[:, :], mparts[:, 0, :], ALU.subtract).then_inc(m_step, 1)
                dve.wait_ge(m_step, 5 * n + 3)
                dve.tensor_copy(mparts[:, 1, :], m2[:, :]).then_inc(m_step, 1)
                dve.wait_ge(m_step, 5 * n + 4)
                dve.tensor_tensor(mparts[:, 2, :], m2[:, :], mparts[:, 1, :], ALU.subtract).then_inc(m_step, 1)

            for blk in range(STEPS):
                reduce_block(0, 0, blk)
            cut_max(0, 0)
            for blk in range(AHEAD):
                reduce_block(1, 1, blk)

            def stage(r, k, nxt, nxt2):
                n = r * 3 + k
                for s in range(STEPS):
                    for off, kk, blk in score_blocks(s, k, nxt, nxt2):
                        reduce_block(n + off, kk, blk)
                        if blk == STEPS - 1:
                            cut_max(n + off, kk)
            stages(dve, stage)


def attend_banded(nc, env, tag):
    STEPS = TB
    FREE_ST, FREE_SC = 3, 2
    AHEAD = 3
    W2 = 2 * BAND
    with ExitStack() as ctx:
        sb = lambda n, s, d: ctx.enter_context(nc.sbuf_tensor(f"{tag}_{n}", s, d))
        ps = lambda n, s, d: ctx.enter_context(nc.psum_tensor(f"{tag}_{n}", s, d))
        sem = lambda n: ctx.enter_context(nc.semaphore(f"{tag}_{n}"))
        qs = [sb(f"qs{i}", [P, HG, S], BF16) for i in range(3)]
        ks = [sb(f"ks{i}", [P, HG, S], BF16) for i in range(3)]
        vg = [sb(f"vg{i}", [P, TB, HG, VW], F32) for i in range(3)]
        prob = [sb(f"prob{i}", [P, W2], F32) for i in range(4)]
        m1 = [sb(f"m1{i}", [P, HG, TB], F32) for i in range(3)]
        m2 = sb("m2", [P, HG * TB], F32)
        mparts = sb("mparts", [P, 3, HG * TB], BF16)
        mt = sb("mt", [3 * HG * TB, P], BF16)
        sc = [ps(f"sc{i}", [P, W2], F32) for i in range(2)]
        st = [ps(f"st{i}", [P, W2], F32) for i in range(3)]
        pv = [ps(f"pv{i}", [P, CH], F32) for i in range(2)]
        turn = ps("turn", [P, 2 * CH], BF16)
        loaded = [sem(f"loaded{i}") for i in range(3)]
        (q_init, v_init, cleared, v_ready, sc_done, red_done, m_step, turned, m_copied, max_ready,
         st_done, exp_done, pv_done, u_out) = map(sem, (
            "q_init", "v_init", "cleared", "v_ready", "sc_done", "red_done", "m_step", "turned", "m_copied",
            "max_ready", "st_done", "exp_done", "pv_done", "u_out"))
        block = ctx.enter_context(nc.Block())
        mask_q, mask_q0, mask_k = env.masks

        Q_INIT = 4 * 3
        LOOPED = 6

        def stages(eng, stage):
            with eng.Fori(0, LOOPED // 3) as i:
                for k in range(3):
                    stage(i, k, True, True)
            stage(LOOPED // 3, 0, True, False)
            stage(LOOPED // 3, 1, False, False)

        def score_blocks(s, k, nxt, nxt2):
            if s < STEPS - AHEAD:
                return [(1, (k + 1) % 3, s + AHEAD)] if nxt else []
            return [(2, (k + 2) % 3, s - (STEPS - AHEAD))] if nxt2 else []

        @block.sync
        def _(sp):
            def load(n, k):
                for t, w in ((qs[k], 0), (ks[k], 1)):
                    sp.dma_start(t[0:SR, :, :].rearrange("p j t -> p (j t)"),
                                 env.stackn[w, n, :, :]).then_inc(loaded[k], 16)

            def max_rows(n, k):
                sp.wait_ge(m_copied, n + 1)
                sp.sem_inc(env.sp_passed, 1)
                for i in range(3):
                    sp.dma_start(qs[k][MAXROW + i:MAXROW + i + 1, :, :].rearrange("p j t -> p (j t)"),
                                 mt[HG * TB * i:HG * TB * (i + 1), :]).then_inc(max_ready, 16)

            sp.wait_ge(q_init, Q_INIT)
            for n in range(2):
                load(n, n)
            max_rows(0, 0)

            def stage(r, k, nxt, nxt2):
                n = r * 3 + k
                if nxt2:
                    sp.wait_ge(st_done, n * 2 * STEPS)
                    sp.sem_inc(env.sp_passed, 1)
                    load(n + 2, (k + 2) % 3)
                if nxt:
                    max_rows(n + 1, (k + 1) % 3)
            stages(sp, stage)

        @block.gpsimd
        def _(pool):
            for k in range(3):
                pool.memset(ks[k][MAXROW:P, :, :], 1.0).then_inc(q_init, 1)
            pool.drain()
            for k in range(3):
                pool.memset(vg[k][:, :, :, :], 1.0).then_inc(v_init, 1)

            def copy_v(n, k):
                pool.tensor_copy(vg[k][:, :, :, 0:HD],
                                 env.vn[:, bass.ds(n, 1), :, :].rearrange("p o t (j d) -> p (o t) j d", j=HG)
                                 ).then_inc(v_ready, 1)

            pool.wait_ge(v_init, 3)
            copy_v(0, 0)
            pool.wait_ge(q_init, Q_INIT)

            def stage(r, k, nxt, nxt2):
                n = r * 3 + k
                if nxt2:
                    pool.wait_ge(st_done, n * 2 * STEPS)
                    pool.wait_ge(v_ready, n + 1)
                    pool.sem_inc(env.pool_passed, 1)
                    pool.memset(qs[(k + 2) % 3][MAXROW:MAXROW + 3, :, :].bitcast(U32), 0).then_inc(cleared, 1)
                    pool.wait_ge(cleared, n + 1)
                if nxt:
                    pool.wait_ge(pv_done, n * STEPS)
                    pool.sem_inc(env.pool_passed, 1)
                    copy_v(n + 1, (k + 1) % 3)
            stages(pool, stage)

        @block.tensor
        def _(pe):
            def scores(n, k, qt):
                mask = mask_q if qt else mask_q0
                for pr in range(2):
                    pe.wait_ge(red_done, n * 2 * STEPS + 2 * qt + pr + 1)
                    pe.matmul(sc[pr][:, :], env.ident16[:, :], mask[:, :], start=True, stop=True)
                    for h in range(2):
                        j = 2 * pr + h
                        first = 0 if qt else WIN
                        mm = pe.matmul(sc[pr][:, h * BAND + first:(h + 1) * BAND], qs[k][:, j, qt * P:(qt + 1) * P],
                                       ks[k][:, j, qt * P - WIN + first:(qt + 1) * P], start=False, stop=True,
                                           skip_group_check=True)
                    mm.then_inc(sc_done, 1)

            def weigh(n, k, s):
                pe.wait_ge(exp_done, FREE_ST + n * 2 * STEPS + 2 * s + 2)
                if s == 0:
                    pe.wait_ge(u_out, n * 2)
                if s == 3:
                    pe.wait_ge(u_out, n * 2)
                spans = {3: ((0, P), (P, BAND)), 7: ((0, P),)}.get(s, ((0, BAND),))
                for a, b in spans:
                    q0 = s * P + a
                    for j in range(HG):
                        mm = pe.matmul(pv[q0 // CH][32 * j:32 * j + 32, q0 % CH:q0 % CH + b - a], vg[k][:, s, j, :],
                                       prob[(2 * s + j // 2) % 4][:, (j % 2) * BAND + a:(j % 2) * BAND + b],
                                       start=s == 0 or (s == 3 and a > 0), stop=True,
                                       skip_group_check=True)
                mm.then_inc(pv_done, 1)

            def turn_max(n):
                pe.wait_ge(m_step, 4 * n + 4)
                pe.transpose(turn[0:3 * HG * TB, 0:P], mparts[:, :, :].rearrange("p a m -> p (a m)"),
                             env.ident16[:, :]).then_inc(turned, 1)

            for n in range(2):
                pe.wait_ge(loaded[n], 32)
                pe.wait_ge(q_init, Q_INIT)
                for qt in range(STEPS if n == 0 else AHEAD):
                    scores(n, n, qt)
                if n == 0:
                    turn_max(0)

            def stage(r, k, nxt, nxt2):
                n = r * 3 + k
                pe.wait_ge(max_ready, 48 * n + 48)
                pe.wait_ge(v_ready, n + 1)
                for s in range(STEPS):
                    width = BAND if s < STEPS - 1 else P
                    if s == STEPS - AHEAD and nxt2:
                        pe.wait_ge(loaded[(k + 2) % 3], (r + (k + 2) // 3) * 32 + 32)
                        pe.wait_ge(cleared, n + 1)
                    for pr in range(2):
                        e = 2 * s + pr
                        bank = st[(k + e) % 3]
                        pe.wait_ge(exp_done, n * 2 * STEPS + e + 1)
                        pe.matmul(bank[:, :], env.ident16[:, :], mask_k[:, :], start=True, stop=True)
                        for h in range(2):
                            j = 2 * pr + h
                            mm = pe.matmul(bank[:, h * BAND:h * BAND + width], ks[k][:, j, s * P:(s + 1) * P],
                                           qs[k][:, j, s * P:s * P + width], start=False, stop=True,
                                           skip_group_check=True)
                        mm.then_inc(st_done, 1)
                    for off, kk, qt in score_blocks(s, k, nxt, nxt2):
                        scores(n + off, kk, qt)
                    if s:
                        weigh(n, k, s - 1)
                    if s == STEPS - AHEAD + 1 and nxt:
                        turn_max(n + 1)
                weigh(n, k, STEPS - 1)
            stages(pe, stage)

        @block.scalar
        def _(act):
            act.sem_inc(exp_done, FREE_ST)

            def copy_max(n):
                act.wait_ge(turned, n + 1)
                if not (isinstance(n, int) and n == 0):
                    act.wait_ge(max_ready, n * 48)
                act.copy(mt[:, :], turn[0:3 * HG * TB, 0:P]).then_inc(m_copied, 1)

            copy_max(0)

            def stage(r, k, nxt, nxt2):
                n = r * 3 + k
                for s in range(STEPS):
                    if s >= 2:
                        act.wait_ge(pv_done, n * STEPS + s - 1)
                    for pr in range(2):
                        e = 2 * s + pr
                        act.wait_ge(st_done, n * 2 * STEPS + e + 1)
                        act.activation(prob[e % 4][:, :], st[(k + e) % 3][:, :], ACT.Exp,
                                       scale=SCALE).then_inc(exp_done, 1)
                    if s in (TB // 2, STEPS - 1):
                        half = 0 if s == TB // 2 else 1
                        act.wait_ge(pv_done, n * STEPS + TB // 2 * (half + 1))
                        act.copy(env.u[:, bass.ds(n, 1), half * CH:(half + 1) * CH].rearrange("p o c -> p (o c)"),
                                 pv[half][:, :]).then_inc(u_out, 1)
                    if s == STEPS - AHEAD + 1 and nxt:
                        copy_max(n + 1)
            stages(act, stage)

        @block.vector
        def _(dve):
            for k in range(3):
                for a, b in ((32, 64), (64, P)):
                    dve.memset(qs[k][a:b, :, :].bitcast(U32), 0).then_inc(q_init, 1)
                dve.memset(ks[k][32:MAXROW, :, :].bitcast(U32), 0).then_inc(q_init, 1)
            dve.sem_inc(red_done, FREE_SC)

            def reduce_tile(n, k, qt):
                for pr in range(2):
                    dve.wait_ge(sc_done, n * 2 * STEPS + 2 * qt + pr + 1)
                    dve.tensor_reduce(m1[k][:, 2 * pr:2 * pr + 2, qt], sc[pr][:, :].rearrange("p (h r) -> p h r", h=2),
                                      AX.X, ALU.max, negate=True).then_inc(red_done, 1)

            def cut_max(n, k):
                m = m1[k][:, :, :].rearrange("p j t -> p (j t)")
                dve.wait_ge(red_done, FREE_SC + (n + 1) * 2 * STEPS)
                if not (isinstance(n, int) and n == 0):
                    dve.wait_ge(turned, n)
                dve.tensor_copy(mparts[:, 0, :], m).then_inc(m_step, 1)
                dve.wait_ge(m_step, 4 * n + 1)
                dve.tensor_tensor(m2[:, :], m, mparts[:, 0, :], ALU.subtract).then_inc(m_step, 1)
                dve.wait_ge(m_step, 4 * n + 2)
                dve.tensor_copy(mparts[:, 1, :], m2[:, :]).then_inc(m_step, 1)
                dve.wait_ge(m_step, 4 * n + 3)
                dve.tensor_tensor(mparts[:, 2, :], m2[:, :], mparts[:, 1, :], ALU.subtract).then_inc(m_step, 1)

            for qt in range(STEPS):
                reduce_tile(0, 0, qt)
            cut_max(0, 0)
            for qt in range(AHEAD):
                reduce_tile(1, 1, qt)

            def stage(r, k, nxt, nxt2):
                n = r * 3 + k
                for s in range(STEPS):
                    for off, kk, qt in score_blocks(s, k, nxt, nxt2):
                        reduce_tile(n + off, kk, qt)
                        if qt == STEPS - 1:
                            cut_max(n + off, kk)
            stages(dve, stage)


def project_out(nc, env, tag):
    with ExitStack() as ctx:
        sb = lambda n, s, d: ctx.enter_context(nc.sbuf_tensor(f"{tag}_{n}", s, d))
        ps = lambda n, s, d: ctx.enter_context(nc.psum_tensor(f"{tag}_{n}", s, d))
        sem = lambda n: ctx.enter_context(nc.semaphore(f"{tag}_{n}"))
        rden = sb("rden", [P, NT, H], F32)
        att = sb("att", [P, 2, C], F32)
        attT = sb("attT", [P, 2, C], F32)
        xb = sb("xb", [P, NT, C], F32)
        ut = [ps(f"ut{i}", [P, CH], F32) for i in range(3)]
        at = [ps(f"at{i}", [P, P], F32) for i in range(2)]
        out = [ps(f"out{i}", [P, C], F32) for i in range(2)]
        ut_done, rden_ready, att_ready, at_done, attT_ready, out_done, xb_ready, x_ready = map(sem, (
            "ut_done", "rden_ready", "att_ready", "at_done", "attT_ready", "out_done", "xb_ready", "x_ready"))
        block = ctx.enter_context(nc.Block())

        @block.tensor
        def _(pe):
            def turn(t):
                if t >= 3:
                    pe.wait_ge(att_ready, t - 2)
                for g in range(G):
                    mm = pe.transpose(ut[t % 3][:, g * P:(g + 1) * P],
                                      env.u[:, G * (t // TB) + g, (t % TB) * P:(t % TB + 1) * P], env.ident[:, :])
                mm.then_inc(ut_done, 1)

            def turn_back(t):
                pe.wait_ge(att_ready, t + 1)
                if t >= 2:
                    pe.wait_ge(attT_ready, t - 1)
                pe.transpose(at[t % 2][:, :], att[:, t % 2, :], env.ident[:, :]).then_inc(at_done, 1)

            def project(t):
                pe.wait_ge(attT_ready, t + 1)
                if t >= 2:
                    pe.wait_ge(x_ready, t - 1)
                pe.matmul(out[t % 2][:, :], attT[:, t % 2, :], env.wo[:, :], start=True, stop=True).then_inc(out_done, 1)

            turn(0)
            turn(1)
            for t in range(NT):
                if t + 2 < NT:
                    turn(t + 2)
                turn_back(t)
                if t:
                    project(t - 1)
            project(NT - 1)

        @block.scalar
        def _(act):
            for t in range(NT):
                act.wait_ge(at_done, t + 1)
                if t >= 2:
                    act.wait_ge(out_done, t - 1)
                act.copy(attT[:, t % 2, :], at[t % 2][:, :]).then_inc(attT_ready, 1)

        @block.vector
        def _(dve):
            dve.tensor_tensor(xb[:, :, :], env.x[:, :, :],
                              env.bo[:, :].rearrange("p (a c) -> p a c", a=1).to_broadcast([P, NT, C]),
                              ALU.add).then_inc(xb_ready, 1)
            dve.wait_ge(xb_ready, 1)

            def divide(t):
                heads = ut[t % 3][:, :].rearrange("p (h i) -> p h i", h=H)
                dve.wait_ge(ut_done, t + 1)
                dve.reciprocal(rden[:, t, :], heads[:, :, HD]).then_inc(rden_ready, 1)
                dve.wait_ge(rden_ready, t + 1)
                if t >= 2:
                    dve.wait_ge(at_done, t - 1)
                dve.tensor_tensor(att[:, t % 2, :].rearrange("p (h i) -> p h i", h=H), heads[:, :, 0:HD],
                                  rden[:, t, :].rearrange("p (h i) -> p h i", i=1).to_broadcast([P, H, HD]),
                                  ALU.mult).then_inc(att_ready, 1)

            def add(t):
                dve.wait_ge(out_done, t + 1)
                dve.tensor_tensor(env.x[:, t, :], out[t % 2][:, :], xb[:, t, :], ALU.add).then_inc(x_ready, 1)

            for t in range(NT):
                divide(t)
                if t >= 2:
                    add(t - 2)
            add(NT - 2)
            add(NT - 1)


def set_up(nc, env, d):
    with ExitStack() as ctx:
        sem = lambda n: ctx.enter_context(nc.semaphore(f"setup_{n}"))
        loaded, zeroed, made = map(sem, ("loaded", "zeroed", "made"))
        block = ctx.enter_context(nc.Block())

        @block.sync
        def _(sp):
            n = 0
            for c in range(NC):
                sp.dma_start(env.x[:, 4 * c:4 * c + 4, :], d["x"].rearrange("b s c -> (b s) c").rearrange(
                    "(t p) c -> p t c", p=P)[:, 4 * c:4 * c + 4, :]).then_inc(loaded, 16)
                n += 1
            for a in (env.a, env.b):
                for dst, src in ((a.wqk[:, :, :], d[a.tag + "wqk"]), (a.wv[:, :], d[a.tag + "wv"]),
                                 (a.wo[:, :], d[a.tag + "wo"]),
                                 (a.bqk[:, :], d[a.tag + "bqk"]),
                                 (a.bv[:, :], d[a.tag + "bv"].rearrange("(o c) -> o c", o=1).to_broadcast([P, C])),
                                 (a.bo[:, :], d[a.tag + "bo"].rearrange("(o c) -> o c", o=1).to_broadcast([P, C]))):
                    sp.dma_start(dst, src).then_inc(loaded, 16)
                    n += 1
            for dst, src in ((env.gate[:, :], d["gate"]), (env.gate_bias[:, :], d["gate_bias"].rearrange(
                    "(o c) -> o c", o=1).to_broadcast([P, 64]))):
                sp.dma_start(dst, src).then_inc(loaded, 16)
                n += 1
            sp.wait_ge(loaded, 16 * n)

        @block.gpsimd
        def _(pool):
            for m in (env.ident[:, :], env.ident16[:, :], *(m[:, :] for m in env.masks)):
                pool.memset(m, 0.0).then_inc(zeroed, 1)
            pool.wait_ge(zeroed, 2 + len(env.masks))
            for m in (env.ident, env.ident16):
                pool.affine_select(out=m[:, :], in_=m[:, :], compare_op=ALU.not_equal, fill=1.0, base=0,
                                   pattern=[[-1, P]], channel_multiplier=1).then_inc(made, 1)
            pool.wait_ge(made, 2)

            def keep(m, base, step, multiplier):
                v = m[:, :].rearrange("p (a r) -> p a r", a=2)
                pool.affine_select(out=v, in_=v, compare_op=ALU.is_ge, fill=BARRED, base=base,
                                   pattern=[[0, 2], [step, BAND]], channel_multiplier=multiplier).then_inc(made, 1)

            mq, mq0, mk = env.masks
            for m in (mq, mq0):
                keep(m, -1, 1, -1)
            keep(mk, 0, 1, -1)
            pool.wait_ge(made, 5)
            for m in (mq, mq0):
                keep(m, WIN, -1, 1)
            keep(mk, WIN - 1, -1, 1)
            pool.wait_ge(made, 8)
            keep(mq0, -WIN, 1, 0)
            pool.wait_ge(made, 9)
            pool.memset(env.before[:, :], 1.0).then_inc(made, 1)
            pool.memset(env.fresh[:, :, :], 1.0).then_inc(made, 1)
            pool.wait_ge(made, 11)
            v = env.before[:, :].rearrange("p (g h) -> p g h", g=GROUPS)
            pool.affine_select(out=v, in_=v, compare_op=ALU.is_ge, fill=0.0, base=-1,
                               pattern=[[1, GROUPS], [-1, GROUPS]], channel_multiplier=0).then_inc(made, 1)
            pool.memset(env.fresh[:, :, 0:1], 0.0).then_inc(made, 1)
            pool.wait_ge(made, 13)


def attention(nc, env, a, tag, attend):
    env.wqk, env.bqk, env.wv, env.bv, env.wo, env.bo = a.wqk, a.bqk, a.wv, a.bv, a.wo, a.bo
    with ExitStack() as ctx:
        sb = lambda n, s, d: ctx.enter_context(nc.sbuf_tensor(f"{tag}_{n}", s, d))
        env.u = sb("u", [P, NG, S], F32)
        env.vn = sb("vn", [P, NG, TB, HG * HD], F32)
        with ExitStack() as c2:
            env.xnT = c2.enter_context(nc.sbuf_tensor(f"{tag}_xnT", [P, B * S], F32))

            def finish(act, c, bank):
                return act.copy(env.xnT[:, c * CH:(c + 1) * CH], bank[:, :])
            layer_norm_and_transpose(nc, env, tag + "ln", finish)
            project_qkv(nc, env, tag + "qkv")
        attend(nc, env, tag + "att")
        project_out(nc, env, tag + "out")


E, INTER, GROUPS, TOPG, TOPK = 64, 64, 8, 4, 6
PAIRS = (E + 2) // 2
ROWS = E + 2
ALL = PAIRS * P
EXP_BITS = 0x7F800000
LAST_STEP = 40
HALF_TOP = 2.0 ** 14


def split_weights(nc, env, d):
    with ExitStack() as ctx:
        sb = lambda n, s, t: ctx.enter_context(nc.sbuf_tensor(f"split_{n}", s, t))
        sem = lambda n: ctx.enter_context(nc.semaphore(f"split_{n}"))
        raw = [sb(f"raw{i}", [P, ALL], F32) for i in range(3)]
        cut = sb("cut", [P, PAIRS, 6, P], F16)
        top = sb("top", [P, 3], F32)
        alltop = sb("alltop", [P, 3], F32)
        pow2 = sb("pow2", [P, 3], F32)
        scale = sb("scale", [P, 3], F32)
        loaded = [sem(f"loaded{i}") for i in range(3)]
        topped, reduced, step, high, low, stored = map(sem, ("topped", "reduced", "step", "high", "low", "stored"))
        block = ctx.enter_context(nc.Block())
        PIECE = 11
        pieces = [(i, j) for i in range(3) for j in range(0, PAIRS, PIECE)]

        @block.sync
        def _(sp):
            for i, n in enumerate(("wg", "wu", "wd")):
                sp.dma_start(raw[i][:, :], d[n]).then_inc(loaded[i], 16)
            sp.wait_ge(low, len(pieces))
            for j in range(0, PAIRS, PIECE):
                sp.dma_start(env.wsplit[j:j + PIECE].rearrange("j p n -> p j n"),
                             cut[:, j:j + PIECE, :, :].rearrange("p j a c -> p j (a c)")).then_inc(stored, 16)
            sp.wait_ge(stored, 16 * PAIRS // PIECE)

        @block.gpsimd
        def _(pool):
            pool.wait_ge(topped, 3)
            pool.partition_all_reduce(alltop[:, :], top[:, :], P, bass.bass_isa.ReduceOp.max).then_inc(reduced, 1)

        @block.scalar
        def _(act):
            act.wait_ge(step, 4)
            for i, j in pieces:
                act.activation(cut[:, j:j + PIECE, 2 * i, :], raw[i][:, j * P:(j + PIECE) * P].rearrange(
                    "p (j c) -> p j c", j=PIECE), ACT.Identity, scale=scale[:, i:i + 1]).then_inc(high, 1)

        @block.vector
        def _(dve):
            for i in range(3):
                dve.wait_ge(loaded[i], 16)
                dve.tensor_reduce(top[:, i:i + 1], raw[i][:, :], AX.X, ALU.max,
                                  apply_absolute_value=True).then_inc(topped, 1)
            dve.wait_ge(reduced, 1)
            dve.tensor_scalar(pow2[:, :].bitcast(I32), alltop[:, :].bitcast(I32), EXP_BITS, None,
                              ALU.bitwise_and).then_inc(step, 1)
            dve.wait_ge(step, 1)
            dve.tensor_scalar(pow2[:, :], pow2[:, :], 2.0 ** -60, 1.0 / HALF_TOP, ALU.max, ALU.mult).then_inc(step, 1)
            dve.wait_ge(step, 2)
            dve.reciprocal(scale[:, :], pow2[:, :]).then_inc(step, 1)
            dve.tensor_copy(env.unscale[:, 0:3], pow2[:, :]).then_inc(step, 1)
            dve.wait_ge(step, 4)
            dve.tensor_tensor(env.unscale[:, 3:4], scale[:, 0:1], scale[:, 1:2], ALU.mult).then_inc(step, 1)
            dve.wait_ge(step, 5)
            dve.tensor_scalar(env.unscale[:, 3:4], env.unscale[:, 3:4], 2.0 ** -29, None, ALU.mult).then_inc(step, 1)
            dve.tensor_scalar(env.unscale[:, 4:5], env.unscale[:, 0:1], env.unscale[:, 1:2], 2.0 ** 29,
                              ALU.mult, ALU.mult).then_inc(step, 1)
            dve.wait_ge(step, 7)
            dve.tensor_tensor(env.unscale[:, 4:5], env.unscale[:, 4:5], env.unscale[:, 2:3], ALU.mult).then_inc(step, 1)
            for n, (i, j) in enumerate(pieces):
                dve.wait_ge(high, n + 1)
                dve.scalar_tensor_tensor(cut[:, j:j + PIECE, 2 * i + 1, :], raw[i][:, j * P:(j + PIECE) * P].rearrange(
                    "p (j c) -> p j c", j=PIECE), scale[:, i:i + 1], cut[:, j:j + PIECE, 2 * i, :],
                    ALU.mult, ALU.subtract).then_inc(low, 1)
            dve.wait_ge(step, 8)
            dve.wait_ge(low, len(pieces))


def route(nc, env, tag):
    with ExitStack() as ctx:
        sb = lambda n, s, t: ctx.enter_context(nc.sbuf_tensor(f"{tag}_{n}", s, t))
        ps = lambda n, s, t: ctx.enter_context(nc.psum_tensor(f"{tag}_{n}", s, t))
        sem = lambda n: ctx.enter_context(nc.semaphore(f"{tag}_{n}"))
        full = lambda n: sb(n, [P, NT, E], F32)
        sc, masked, gt, eq, rank, keep, w = map(full, ("sc", "masked", "gt", "eq", "rank", "keep", "w"))
        gs = sb("gs", [P, NT, GROUPS], F32)
        gsel = sb("gsel", [P, NT, GROUPS], F32)
        top8 = sb("top8", [P, NT, 8], F32)
        quota = sb("quota", [P, NT], F32)
        total = sb("total", [P, NT], F32)
        inv = sb("inv", [P, NT], F32)
        comb = sb("comb", [P, NT, ROWS], F32)
        combT = sb("combT", [ROWS, B * S], F32)
        lg = [ps(f"lg{i}", [P, NT // 2, E], F32) for i in range(2)]
        tp = [ps(f"tp{i}", [ROWS, CH], F32) for i in range(2)]
        lg_done, sig_ready, step, turned, copied, stored = map(sem, (
            "lg_done", "sig_ready", "step", "turned", "copied", "stored"))
        xh_ready, xl_ready = map(sem, ("xh_ready", "xl_ready"))
        block = ctx.enter_context(nc.Block())

        @block.tensor
        def _(pe):
            for t in range(NT):
                mm = pe.matmul(lg[t // 8][:, t % 8, :], env.xnT[:, t * P:(t + 1) * P], env.gate[:, :],
                               start=True, stop=True)
                if t % 8 == 7:
                    mm.then_inc(lg_done, 1)
            pe.wait_ge(step, LAST_STEP)
            for t in range(NT):
                c = t // 4
                if c >= 2 and t % 4 == 0:
                    pe.wait_ge(copied, c - 1)
                mm = pe.transpose(tp[c % 2][:, (t % 4) * P:(t % 4 + 1) * P], comb[:, t, :], env.ident[:, :])
                if t % 4 == 3:
                    mm.then_inc(turned, 1)

        @block.scalar
        def _(act):
            for c in range(NC):
                cs = slice(c * CH, (c + 1) * CH)
                act.copy(env.xh[:, cs], env.xnT[:, cs]).then_inc(xh_ready, 1)
            for i in range(2):
                act.wait_ge(lg_done, i + 1)
                act.activation(sc[:, 8 * i:8 * i + 8, :], lg[i][:, :, :], ACT.Sigmoid).then_inc(sig_ready, 1)
            for c in range(NC):
                act.wait_ge(turned, c + 1)
                act.copy(combT[:, c * CH:(c + 1) * CH], tp[c % 2][:, :]).then_inc(copied, 1)

        count = [0]

        @block.gpsimd
        def _(pool):
            for c in range(NC):
                cs = slice(c * CH, (c + 1) * CH)
                pool.wait_ge(xh_ready, c + 1)
                pool.tensor_tensor(env.xl[:, cs], env.xnT[:, cs], env.xh[:, cs], ALU.subtract).then_inc(xl_ready, 1)
            pool.wait_ge(xl_ready, NC)

        @block.vector
        def _(dve):
            def goes_on(ins):
                ins.then_inc(step, 1)
                count[0] += 1

            def done(ins):
                goes_on(ins)
                dve.wait_ge(step, count[0])

            over_e = lambda a: a.rearrange("p (t o) -> p t o", o=1).to_broadcast([P, NT, E])
            dve.wait_ge(sig_ready, 2)
            done(dve.tensor_tensor(sc[:, :, :], sc[:, :, :], env.gate_bias[:, :].rearrange(
                "p (o e) -> p o e", o=1).to_broadcast([P, NT, E]), ALU.add))
            done(dve.tensor_reduce(gs[:, :, :], sc[:, :, :].rearrange("p t (g e) -> p t g e", g=GROUPS), AX.X, ALU.max))
            square = lambda a: a[:, :, :].rearrange("p t (g o) -> p t g o", g=GROUPS)
            mine = gs[:, :, :].rearrange("p t (g o) -> p t g o", o=1).to_broadcast([P, NT, GROUPS, GROUPS])
            other = gs[:, :, :].rearrange("p t (o g) -> p t o g", o=1).to_broadcast([P, NT, GROUPS, GROUPS])
            before = env.before[:, :].rearrange("p (o e) -> p o e", o=1).to_broadcast([P, NT, E])
            dve.tensor_tensor(square(gt), other, mine, ALU.is_gt).then_inc(step, 1)
            count[0] += 1
            done(dve.tensor_tensor(square(eq), other, mine, ALU.is_equal))
            done(dve.tensor_tensor(eq[:, :, :], eq[:, :, :], before, ALU.mult))
            done(dve.tensor_tensor(rank[:, :, :], gt[:, :, :], eq[:, :, :], ALU.add))
            done(dve.tensor_reduce(gsel[:, :, :], square(rank), AX.X, ALU.add))
            done(dve.tensor_scalar(gsel[:, :, :], gsel[:, :, :], float(TOPG), None, ALU.is_lt))
            done(dve.tensor_tensor(square(masked), square(sc), gsel[:, :, :].rearrange(
                "p t (g o) -> p t g o", o=1).to_broadcast([P, NT, GROUPS, GROUPS]), ALU.mult))
            for t in range(NT):
                dve.max(top8[:, t, :], masked[:, t, :]).then_inc(step, 1)
                count[0] += 1
            dve.wait_ge(step, count[0])
            sixth = over_e(top8[:, :, TOPK - 1])
            dve.tensor_tensor(gt[:, :, :], masked[:, :, :], sixth, ALU.is_gt).then_inc(step, 1)
            count[0] += 1
            done(dve.tensor_tensor(eq[:, :, :], masked[:, :, :], sixth, ALU.is_equal))
            done(dve.tensor_reduce(quota[:, :], gt[:, :, :], AX.X, ALU.add))
            dve.tensor_scalar(quota[:, :], quota[:, :], -1.0, float(TOPK), ALU.mult, ALU.add).then_inc(step, 1)
            count[0] += 1
            flat = lambda a: a[:, :, :].rearrange("p t e -> p (t e)")
            done(dve.tensor_tensor_scan(flat(rank), flat(env.fresh), flat(eq), 0.0, ALU.mult, ALU.add))
            done(dve.tensor_tensor(keep[:, :, :], rank[:, :, :], over_e(quota[:, :]), ALU.is_le))
            done(dve.tensor_tensor(keep[:, :, :], keep[:, :, :], eq[:, :, :], ALU.mult))
            done(dve.tensor_tensor(keep[:, :, :], keep[:, :, :], gt[:, :, :], ALU.add))
            done(dve.tensor_tensor(w[:, :, :], keep[:, :, :], masked[:, :, :], ALU.mult))
            done(dve.tensor_reduce(total[:, :], w[:, :, :], AX.X, ALU.add))
            done(dve.tensor_scalar(total[:, :], total[:, :], 1e-8, None, ALU.add))
            done(dve.reciprocal(inv[:, :], total[:, :]))
            done(dve.tensor_scalar(inv[:, :], inv[:, :], env.unscale[:, 3:4], None, ALU.mult))
            dve.tensor_tensor(comb[:, :, 0:E], w[:, :, :], over_e(inv[:, :]), ALU.mult).then_inc(step, 1)
            dve.tensor_copy(comb[:, :, E:ROWS], env.unscale[:, 3:4].rearrange("p (o e) -> p o e", o=1)
                            .to_broadcast([P, NT, 2])).then_inc(step, 1)
            count[0] += 2
            assert count[0] == LAST_STEP

        @block.sync
        def _(sp):
            sp.wait_ge(copied, NC)
            sp.dma_start(env.comb[:, :], combT[:, :]).then_inc(stored, 16)
            sp.wait_ge(stored, 16)


def experts(nc, env, tag):
    QN = PAIRS * NC
    FREE_UP, FREE3 = 2, 3
    BODY = 3 * NC
    ROUNDS = PAIRS // 3
    with ExitStack() as ctx:
        sb = lambda n, s, t: ctx.enter_context(nc.sbuf_tensor(f"{tag}_{n}", s, t))
        ps = lambda n, s, t: ctx.enter_context(nc.psum_tensor(f"{tag}_{n}", s, t))
        sem = lambda n: ctx.enter_context(nc.semaphore(f"{tag}_{n}"))
        wt = [sb(f"wt{i}", [P, 6, P], F16) for i in range(3)]
        cb = [sb(f"cb{i}", [P, B * S], F32) for i in range(3)]
        sil = [sb(f"sil{i}", [P, CH], F32) for i in range(2)]
        act_up = [sb(f"act_up{i}", [P, CH], F32) for i in range(3)]
        hid = [sb(f"hid{i}", [P, CH], F32) for i in range(3)]
        high = [sb(f"high{i}", [P, CH], F16) for i in range(3)]
        low = [sb(f"low{i}", [P, CH], F16) for i in range(3)]
        sums = [sb(f"sums{i}", [P, CH], F32) for i in range(NC)]
        gate = [ps(f"gate{i}", [P, CH], F32) for i in range(2)]
        up = [ps(f"up{i}", [P, CH], F32) for i in range(2)]
        acc = [ps(f"acc{i}", [P, CH], F32) for i in range(NC)]
        wt_in = [sem(f"wt_in{i}") for i in range(3)]
        cb_in = [sem(f"cb_in{i}") for i in range(3)]
        g_done, u_done, sil_ready, up_ready, hid_ready, high_ready, low_ready, down_done = map(sem, (
            "g_done", "u_done", "sil_ready", "up_ready", "hid_ready", "high_ready", "low_ready", "down_done"))
        sum_ready, back_done, x_ready = map(sem, ("sum_ready", "back_done", "x_ready"))
        block = ctx.enter_context(nc.Block())

        def looped(eng, body):
            with eng.Fori(0, ROUNDS - 1) as r:
                for i in range(BODY):
                    body(r * BODY + i, i, r, False)
            for i in range(BODY):
                body((ROUNDS - 1) * BODY + i, i, ROUNDS - 1, True)

        @block.sync
        def _(sp):
            def load(j, k):
                sp.dma_start(wt[k][:, :, :].rearrange("p a c -> p (a c)"), env.wsplit[j, :, :]).then_inc(wt_in[k], 16)
                for e in range(2):
                    sp.dma_start(cb[k][64 * e:64 * e + 64, :],
                                 env.comb2[j, e:e + 1, :].to_broadcast([64, B * S])).then_inc(cb_in[k], 16)
            for k in range(3):
                load(k, k)
            with sp.Fori(0, ROUNDS - 1) as r:
                for k in range(3):
                    sp.wait_ge(down_done, FREE3 + r * BODY + NC * (k + 1))
                    sp.sem_inc(env.sp_passed, 1)
                    load(r * 3 + k + 3, k)

        @block.tensor
        def _(pe):
            def gate_up(q, i, r):
                c, k = i % NC, i // NC % 3
                cs = slice(c * CH, (c + 1) * CH)
                if c == 0:
                    pe.wait_ge(wt_in[k], (r + i // BODY) * 16 + 16)
                pe.wait_ge(up_ready, q + 1)
                for bank, a, done in ((gate, 0, g_done), (up, 2, u_done)):
                    o = bank[i % 2][:, :]
                    pe.matmul(o, wt[k][:, a, :], env.xh[:, cs], start=True, stop=False)
                    pe.matmul(o, wt[k][:, a, :], env.xl[:, cs], start=False, stop=False)
                    pe.matmul(o, wt[k][:, a + 1, :], env.xh[:, cs], start=False, stop=True).then_inc(done, 1)

            def down(q, i, first, last):
                c, k = i % NC, i // NC % 3
                o = acc[c][:, :]
                skip = dict(skip_group_check=True)
                pe.wait_ge(high_ready, q + 1)
                pe.matmul(o, wt[k][:, 4, :], high[i % 3][:, :], start=first, stop=False, **skip)
                pe.matmul(o, wt[k][:, 5, :], high[i % 3][:, :], start=False, stop=False, **skip)
                pe.wait_ge(low_ready, FREE3 + q + 1)
                pe.matmul(o, wt[k][:, 4, :], low[i % 3][:, :], start=False, stop=last, **skip).then_inc(down_done, 1)

            pe.sem_inc(down_done, FREE3)
            for q in range(4):
                gate_up(q, q, 0)
            for i in range(BODY):
                gate_up(i + 4, i + 4, 0)
                down(i, i, i < NC, False)
            with pe.Fori(1, ROUNDS - 1) as r:
                for i in range(BODY):
                    gate_up(r * BODY + i + 4, i + 4, r)
                    down(r * BODY + i, i, False, False)
            for i in range(BODY):
                q = (ROUNDS - 1) * BODY + i
                if q + 4 < QN:
                    gate_up(q + 4, i + 4, ROUNDS - 1)
                down(q, i, False, i >= BODY - NC)
            for c in range(NC):
                pe.wait_ge(sum_ready, c + 1)
                if c >= 2:
                    pe.wait_ge(x_ready, c - 1)
                for t in range(4):
                    mm = pe.transpose(gate[c % 2][:, t * P:(t + 1) * P], sums[c][:, t * P:(t + 1) * P], env.ident[:, :])
                mm.then_inc(back_done, 1)

        @block.scalar
        def _(act):
            def silu(q, i):
                act.wait_ge(g_done, q + 1)
                act.activation(sil[i % 2][:, :], gate[i % 2][:, :], ACT.Silu, scale=env.unscale[:, 0:1]).then_inc(sil_ready, 1)

            def high_part(q, i):
                act.wait_ge(down_done, q + 1)
                act.wait_ge(hid_ready, q + 1)
                act.copy(high[i % 3][:, :], hid[i % 3][:, :]).then_inc(high_ready, 1)

            for q in range(3):
                silu(q, q)
            high_part(0, 0)

            def body(q, i, r, last):
                if not (last and i + 3 >= BODY):
                    silu(q + 3, i + 3)
                if not (last and i + 1 >= BODY):
                    high_part(q + 1, i + 1)
            looped(act, body)
            for c in range(NC):
                act.wait_ge(down_done, FREE3 + QN - NC + c + 1)
                act.activation(sums[c][:, :], acc[c][:, :], ACT.Identity,
                               scale=env.unscale[:, 4:5]).then_inc(sum_ready, 1)

        @block.vector
        def _(dve):
            dve.sem_inc(up_ready, FREE_UP)

            def times_up(q, i):
                dve.wait_ge(sil_ready, q + 1)
                dve.wait_ge(u_done, q + 1)
                dve.scalar_tensor_tensor(act_up[i % 3][:, :], up[i % 2][:, :], env.unscale[:, 1:2], sil[i % 2][:, :],
                                         ALU.mult, ALU.mult).then_inc(up_ready, 1)

            def times_weight(q, i, r):
                c, k = i % NC, i // NC % 3
                if c == 0:
                    dve.wait_ge(cb_in[k], (r + i // BODY) * 32 + 32)
                dve.wait_ge(up_ready, FREE_UP + q + 1)
                dve.wait_ge(low_ready, q + 1)
                dve.tensor_tensor(hid[i % 3][:, :], act_up[i % 3][:, :], cb[k][:, c * CH:(c + 1) * CH],
                                  ALU.mult).then_inc(hid_ready, 1)

            times_up(0, 0)
            times_up(1, 1)
            times_weight(0, 0, 0)

            def body(q, i, r, last):
                if not (last and i + 2 >= BODY):
                    dve.wait_ge(hid_ready, q)
                    times_up(q + 2, i + 2)
                if not (last and i + 1 >= BODY):
                    times_weight(q + 1, i + 1, r)
            looped(dve, body)

            for c in range(NC):
                dve.wait_ge(back_done, c + 1)
                xs = env.x[:, 4 * c:4 * c + 4, :].rearrange("p t c -> p (t c)")
                dve.tensor_tensor(xs, xs, gate[c % 2][:, :], ALU.add).then_inc(x_ready, 1)

        @block.gpsimd
        def _(pool):
            pool.sem_inc(low_ready, FREE3)

            def body(q, i, r, last):
                pool.wait_ge(high_ready, q + 1)
                pool.wait_ge(down_done, q + 1)
                pool.tensor_tensor(low[i % 3][:, :], hid[i % 3][:, :], high[i % 3][:, :], ALU.subtract).then_inc(low_ready, 1)
            looped(pool, body)


def moe(nc, env, tag):
    with ExitStack() as ctx:
        env.xh = ctx.enter_context(nc.sbuf_tensor(f"{tag}_xh", [P, B * S], F16))
        env.xl = ctx.enter_context(nc.sbuf_tensor(f"{tag}_xl", [P, B * S], F16))
        with ExitStack() as c2:
            env.xnT = c2.enter_context(nc.sbuf_tensor(f"{tag}_xnT", [P, B * S], F32))

            def finish(act, c, bank):
                return act.copy(env.xnT[:, c * CH:(c + 1) * CH], bank[:, :])
            layer_norm_and_transpose(nc, env, tag + "ln", finish)
            route(nc, env, tag + "rt")
        experts(nc, env, tag + "ex")


def transformer(nc, d, out):
    env = Env()
    with ExitStack() as ctx:
        sb = lambda n, s, t: ctx.enter_context(nc.sbuf_tensor(n, s, t))
        env.x = sb("x_res", [P, NT, C], F32)
        env.ident = sb("ident", [P, P], F32)
        env.ident16 = sb("ident16", [P, P], BF16)
        env.masks = [sb(f"mask{i}", [P, 2 * BAND], BF16) for i in range(3)]
        env.gate = sb("gate", [P, E], F32)
        env.gate_bias = sb("gate_bias", [P, E], F32)
        env.before = sb("before", [P, E], F32)
        env.fresh = sb("fresh", [P, NT, E], F32)
        env.unscale = sb("unscale", [P, 5], F32)
        env.a, env.b = Env(), Env()
        for tag, a in (("a", env.a), ("b", env.b)):
            a.tag = tag
            a.wqk = sb(tag + "_wqk", [P, 2, C], F32)
            a.bqk = sb(tag + "_bqk", [P, 2], F32)
            a.wv = sb(tag + "_wv", [P, C], F32)
            a.bv = sb(tag + "_bv", [P, C], F32)
            a.wo = sb(tag + "_wo", [P, C], F32)
            a.bo = sb(tag + "_bo", [P, C], F32)
        env.sp_passed, env.pool_passed = (ctx.enter_context(nc.semaphore(n)) for n in ("sp_passed", "pool_passed"))
        env.stack = nc.dram_tensor("stack", [2, B, G, SLOTS, HD, HG, S], BF16).ap()
        env.stackn = env.stack.rearrange("w b g r d j t -> w (b g) (r d) (j t)")
        env.wsplit = nc.dram_tensor("wsplit", [PAIRS, P, 6 * P], F16).ap()
        env.comb = nc.dram_tensor("comb", [ROWS, B * S], F32).ap()
        env.comb2 = env.comb.rearrange("(j e) t -> j e t", e=2)

        set_up(nc, env, d)
        split_weights(nc, env, d)
        attention(nc, env, env.a, "A", attend_full)
        moe(nc, env, "M1")
        attention(nc, env, env.b, "B", attend_banded)
        moe(nc, env, "M2")

        out_done = ctx.enter_context(nc.semaphore("out_done"))
        block = ctx.enter_context(nc.Block())

        @block.sync
        def _(sp):
            sp.dma_start(out.rearrange("b s c -> (b s) c").rearrange("(t p) c -> p t c", p=P),
                         env.x[:, :, :]).then_inc(out_done, 16)
            sp.wait_ge(out_done, 16)


def lay_out(np, inputs):
    get = lambda n: np.asarray(inputs["L0_" + n])
    by_width = lambda a: a.reshape(-1, G, HG, HD).transpose(0, 1, 3, 2).reshape(-1, C)
    d = {"x": get("attn_a_x")}
    for w in "ab":
        wq, wk, wv, wo = (get(f"attn_{w}_{n}") for n in ("Wq", "Wk", "Wv", "Wo"))
        if w == "a":
            wq, wk, wv, wo = wq.T, wk.T, wv.T, wo.T
        d[w + "wqk"] = np.stack([by_width(wq), by_width(wk)], 1)
        d[w + "bqk"] = np.stack([by_width(get(f"attn_{w}_bq"))[0], by_width(get(f"attn_{w}_bk"))[0]], 1)
        d[w + "wv"], d[w + "wo"] = wv, wo
        d[w + "bv"], d[w + "bo"] = get(f"attn_{w}_bv"), get(f"attn_{w}_bo")
    rows = lambda experts, shared: np.concatenate([experts.reshape(-1, C), shared], 0)
    d["wg"] = rows(get("ffn_eg_w"), get("ffn_sg_w")).T
    d["wu"] = rows(get("ffn_eu_w"), get("ffn_su_w")).T
    down = rows(get("ffn_ed_w").transpose(0, 2, 1), get("ffn_sd_w").T)
    d["wd"] = down.reshape(PAIRS, P, C).transpose(1, 0, 2).reshape(P, -1)
    d["gate"] = get("ffn_gate_w").T
    d["gate_bias"] = get("ffn_gate_bias")
    return {n: np.ascontiguousarray(a) for n, a in d.items()}


def kernel(**inputs):
    import numpy as np
    import concourse.bacc as bacc
    from concourse.bass_utils import run_bass_kernel_spmd

    nc = bacc.Bacc("TRN2", target_bir_lowering=False, num_devices=1)
    arrays, d = {}, {}
    for name, a in lay_out(np, inputs).items():
        arrays[f"in_{name}_dram"] = a
        d[name] = nc.dram_tensor(f"in_{name}_dram", a.shape, mybir.dt.from_np(a.dtype), kind="ExternalInput").ap()
    out = nc.dram_tensor("out_0_dram", (B, S, C), F32, kind="ExternalOutput").ap()
    transformer(nc, d, out)
    r = run_bass_kernel_spmd(nc, [arrays], core_ids=[0])
    return r.results[0]["out_0_dram"]
```

```python
from contextlib import ExitStack

import concourse.bass as bass
from concourse import mybir

F32 = mybir.dt.float32
BF16 = mybir.dt.bfloat16
F16 = mybir.dt.float16
I32 = mybir.dt.int32
U32 = mybir.dt.uint32
ACT = mybir.ActivationFunctionType
ALU = mybir.AluOpType
AX = mybir.AxisListType

P = 128
B, S, C = 2, 1024, 128
NT = B * S // P
TB = S // P
H, HD = 16, 8
HG = 4
G = H // HG
NG = B * G
CH = 512
NC = B * S // CH
SLOTS = 6
RUNS = ((0, 3, 0, 0), (3, 2, 0, 1), (5, 1, 0, 2))
STORES = 16 * 2 * G
LOADS = 16 * 2 * len(RUNS)
SR = SLOTS * HD
MAXROW = 64
VW = 32
WIN = 32
BAND = P + WIN
BARRED = -1e30
EPS = 1e-5
SCALE = float(HD) ** -0.5


class Env:
    pass


def semaphore(nc, env, name):
    env.semaphores.append(nc.alloc_semaphore(name))
    return env.semaphores[-1]


def end_of_layer(nc, env):
    nc.clear_and_free_semaphores(env.semaphores)
    nc.all_engine_barrier()
    env.semaphores = []


def layer_norm(nc, ctx, env, tag):
    sb = lambda n, s: ctx.enter_context(nc.sbuf_tensor(f"{tag}_{n}", s, F32))
    w = Env()
    w.stats = sb("stats", [P, NT, 6])
    w.mv = sb("mv", [P, NT, 2])
    w.ve, w.sd, w.r0, w.r1, w.rstd = (sb(n, [P, NT]) for n in ("ve", "sd", "r0", "r1", "rstd"))
    w.xn = sb("xn", [P, NT, C])
    w.tp = [ctx.enter_context(nc.psum_tensor(f"{tag}_tp{i}", [P, CH], F32)) for i in range(2)]
    w.step, w.var_ready, w.sd_ready, w.xn_ready, w.turned, w.copied = (semaphore(nc, env, f"{tag}_{n}") for n in (
        "step", "var_ready", "sd_ready", "xn_ready", "turned", "copied"))
    return w


def norm_vector(dve, env, w):
    for t in range(NT):
        dve.bn_stats(w.stats[:, t, :], env.x[:, t, :]).then_inc(w.step, 1)
    dve.wait_ge(w.step, NT)
    for t in range(NT):
        dve.bn_aggr(w.mv[:, t, :], w.stats[:, t, :]).then_inc(w.step, 1)
    dve.wait_ge(w.step, 2 * NT)
    dve.tensor_scalar(w.ve[:, :], w.mv[:, :, 1], EPS, None, ALU.add).then_inc(w.var_ready, 1)
    dve.wait_ge(w.sd_ready, 1)
    dve.reciprocal(w.r0[:, :], w.sd[:, :]).then_inc(w.step, 1)
    dve.wait_ge(w.step, 2 * NT + 1)
    dve.tensor_tensor(w.r1[:, :], w.r0[:, :], w.r0[:, :], ALU.mult).then_inc(w.step, 1)
    dve.wait_ge(w.step, 2 * NT + 2)
    dve.scalar_tensor_tensor(w.r1[:, :], w.r1[:, :], -0.5, w.ve[:, :], ALU.mult, ALU.mult).then_inc(w.step, 1)
    dve.wait_ge(w.step, 2 * NT + 3)
    dve.scalar_tensor_tensor(w.rstd[:, :], w.r1[:, :], 1.5, w.r0[:, :], ALU.add, ALU.mult).then_inc(w.step, 1)
    dve.wait_ge(w.step, 2 * NT + 4)
    for t in range(NT):
        dve.tensor_scalar(w.xn[:, t, :], env.x[:, t, :], w.mv[:, t, 0:1], w.rstd[:, t:t + 1],
                          ALU.subtract, ALU.mult).then_inc(w.xn_ready, 1)


def norm_tensor(pe, env, w):
    for t in range(NT):
        c = t // 4
        if c >= 2 and t % 4 == 0:
            pe.wait_ge(w.copied, c - 1)
        pe.wait_ge(w.xn_ready, t + 1)
        pe.transpose(w.tp[c % 2][:, (t % 4) * P:(t % 4 + 1) * P], w.xn[:, t, :], env.ident[:, :]).then_inc(w.turned, 1)


def norm_scalar(act, env, w):
    act.wait_ge(w.var_ready, 1)
    act.activation(w.sd[:, :], w.ve[:, :], ACT.Sqrt).then_inc(w.sd_ready, 1)
    for c in range(NC):
        act.wait_ge(w.turned, 4 * (c + 1))
        act.copy(env.xnT[:, c * CH:(c + 1) * CH], w.tp[c % 2][:, :]).then_inc(w.copied, 1)


def project_qkv(nc, env, tag, first):
    with ExitStack() as ctx:
        sb = lambda n, s, d: ctx.enter_context(nc.sbuf_tensor(f"{tag}_{n}", s, d))
        sem = lambda n: semaphore(nc, env, f"{tag}_{n}")
        full = sb("full", [P, 4, CH], F32)
        rest = sb("rest", [P, 4, CH], F32)
        part = sb("part", [P, 2, 3, B * S], BF16)
        HIGH, MID, LOW = (0, 2), (1, 1), (2, 0)
        pq = [ctx.enter_context(nc.psum_tensor(f"{tag}_pq{i}", [P, CH], F32)) for i in range(4)]
        pv = [ctx.enter_context(nc.psum_tensor(f"{tag}_pv{i}", [P, CH], F32)) for i in range(2)]
        mm_done, v_done, full_ready, high_ready, rest_ready, mid_ready, low_ready, v_out = map(sem, (
            "mm_done", "v_done", "full_ready", "high_ready", "rest_ready", "mid_ready", "low_ready", "v_out"))
        constants_set = sem("constants_set")
        norm = layer_norm(nc, ctx, env, tag + "ln")
        block = ctx.enter_context(nc.Block())
        ORDER = [(w, c) for b in range(B) for w in range(2) for c in range(b * NC // B, (b + 1) * NC // B)]

        @block.tensor
        def _(pe):
            norm_tensor(pe, env, norm)

            def values(t0, t1):
                for t in range(t0, t1):
                    if t >= 8 and t % 4 == 0:
                        pe.wait_ge(v_out, t // 4 - 1)
                    pe.matmul(pv[t // 4 % 2][:, (t % 4) * P:(t % 4 + 1) * P], env.xnT[:, t * P:(t + 1) * P],
                              env.wv[:, :], start=True, stop=True).then_inc(v_done, 1)

            for n, (w, c) in enumerate(ORDER):
                if n == len(ORDER) // 2:
                    values(0, NT // 2)
                pe.wait_ge(norm.copied, c + 1)
                if n >= 4:
                    pe.wait_ge(full_ready, n - 3)
                pe.matmul(pq[n % 4][:, :], env.wqk[:, w, :], env.xnT[:, c * CH:(c + 1) * CH],
                          start=True, stop=True).then_inc(mm_done, 1)
            values(NT // 2, NT)

        @block.scalar
        def _(act):
            norm_scalar(act, env, norm)

            def middle(n):
                w, c = ORDER[n]
                act.wait_ge(rest_ready, n + 1)
                act.copy(part[:, w, MID[w], c * CH:(c + 1) * CH], rest[:, n % 4, :]).then_inc(mid_ready, 1)

            for n, (w, c) in enumerate(ORDER):
                act.wait_ge(mm_done, n + 1)
                if n >= 4:
                    act.wait_ge(low_ready, n - 3)
                act.activation(full[:, n % 4, :], pq[n % 4][:, :], ACT.Identity,
                               bias=env.bqk[:, w:w + 1]).then_inc(full_ready, 1)
                act.wait_ge(full_ready, n + 1)
                act.copy(part[:, w, HIGH[w], c * CH:(c + 1) * CH], full[:, n % 4, :]).then_inc(high_ready, 1)
                if n:
                    middle(n - 1)
            middle(len(ORDER) - 1)

        @block.vector
        def _(dve):
            norm_vector(dve, env, norm)

            def low(n):
                w, c = ORDER[n]
                cs = slice(c * CH, (c + 1) * CH)
                dve.wait_ge(mid_ready, n + 1)
                dve.tensor_tensor(part[:, w, LOW[w], cs], rest[:, n % 4, :], part[:, w, MID[w], cs], ALU.subtract).then_inc(low_ready, 1)

            for n, (w, c) in enumerate(ORDER):
                cs = slice(c * CH, (c + 1) * CH)
                dve.wait_ge(high_ready, n + 1)
                dve.tensor_tensor(rest[:, n % 4, :], full[:, n % 4, :], part[:, w, HIGH[w], cs], ALU.subtract).then_inc(rest_ready, 1)
                if n:
                    low(n - 1)
            low(len(ORDER) - 1)
            for c in range(NC):
                dve.wait_ge(v_done, 4 * (c + 1))
                bias = env.bv[:, :].rearrange("p (a g c) -> p a g c", a=1, g=G).to_broadcast([P, 4, G, HG * HD])
                b, k = c // 2, c % 2
                dve.tensor_tensor(env.vn[:, G * b:G * b + G, 4 * k:4 * k + 4, :].rearrange("p g a c -> p a g c"),
                                  pv[c % 2][:, :].rearrange("p (a g c) -> p a g c", a=4, g=G),
                                  bias, ALU.add).then_inc(v_out, 1)

        @block.sync
        def _(sp):
            for b in range(B):
                for w in range(2):
                    sp.wait_ge(low_ready, (2 * b + w + 1) * NC // B)
                    for g in range(G):
                        sp.dma_start(env.stack[w, b * G + g].rearrange("s r t -> r s t"),
                                     part[32 * g:32 * g + 32, w, :, b * S:(b + 1) * S]).then_inc(env.stored[b], 16)
                if b == 0:
                    sp.wait_ge(env.stored[0], STORES)
                    sp.wait_ge(env.q_cleared, 3)
                    if first:
                        sp.wait_ge(constants_set, len(ZERO_ROWS) - 4)
                    load_group(sp, env, 0, 0)

        @block.gpsimd
        def _(pool):
            for k in range(3):
                pool.memset(env.qs[k][MAXROW:MAXROW + 3, :, :].bitcast(U32), 0).then_inc(env.q_cleared, 1)
            if first:
                pool.drain()
                for t, a, b in ZERO_ROWS[4:]:
                    pool.memset(env.stacks[t][a:b, :, :].bitcast(U32), 0).then_inc(constants_set, 1)
                pool.drain()
                for k in range(3):
                    pool.memset(env.ks[k][MAXROW:P, :, :], 1.0).then_inc(constants_set, 1)
                pool.drain()
                for k in range(3):
                    pool.memset(env.vg[k][:, :, :, :], 1.0).then_inc(constants_set, 1)
                pool.wait_ge(constants_set, 6 + len(ZERO_ROWS) - 4)


def load_group(sp, env, n, k):
    for slot, slots, *part in RUNS:
        for t, w in ((env.qs[k], 0), (env.ks[k], 1)):
            sp.dma_start(t[slot * HD:(slot + slots) * HD, :, :].rearrange("p j t -> p (j t)"),
                         env.stackn[w, n, part[w] * HD:(part[w] + slots) * HD, :]).then_inc(env.loaded[k], 16)


def attend_full(nc, env, tag):
    STEPS = 2 * TB
    FREE = 2
    FREE_SC = 3
    ONE = 1
    AHEAD = 4
    NS = 4 * STEPS
    with ExitStack() as ctx:
        sb = lambda n, s, d: ctx.enter_context(nc.sbuf_tensor(f"{tag}_{n}", s, d))
        ps = lambda n, s, d: ctx.enter_context(nc.psum_tensor(f"{tag}_{n}", s, d))
        sem = lambda n: semaphore(nc, env, f"{tag}_{n}")
        qs, ks, vg, loaded = env.qs, env.ks, env.vg, env.loaded
        prob = [sb(f"prob{i}", [P, 2, CH], F32) for i in range(4)]
        mx = [sb(f"mx{i}", [P, HG * TB, 2], F32) for i in range(3)]
        m1 = sb("m1", [P, HG * TB], F32)
        m2 = sb("m2", [P, HG * TB], F32)
        mparts = sb("mparts", [P, 3, HG * TB], BF16)
        mt = sb("mt", [3 * HG * TB, P], BF16)
        sc = [ps(f"sc{i}", [P, CH], F32) for i in range(3)]
        st = [ps(f"st{i}", [P, 2, CH], F32) for i in range(2)]
        pv = ps("pv", [P, CH], F32)
        (cleared, v_ready, sc_done, red_done, m_step, turned, m_copied, max_ready,
         st_done, exp_done, pv_done, u_out) = map(sem, (
            "cleared", "v_ready", "sc_done", "red_done", "m_step", "turned", "m_copied",
            "max_ready", "st_done", "exp_done", "pv_done", "u_out"))
        weights = splitter(nc, ctx, env, env.sources)
        block = ctx.enter_context(nc.Block())

        LOOPED = 6

        def stages(eng, stage):
            with eng.Fori(0, LOOPED // 3) as i:
                for k in range(3):
                    stage(i, k, True, True)
            stage(LOOPED // 3, 0, True, False)
            stage(LOOPED // 3, 1, False, False)

        def sc_bank(k, i):
            return sc[(NS * k + i) % 3]

        TURN_TILE = 4 * 1

        def turn_bank(k):
            return sc_bank((k + 1) % 3, TURN_TILE)[:, :].bitcast(BF16)[0:3 * HG * TB, 0:P]

        def score_blocks(s, k, nxt, nxt2):
            if s < STEPS - AHEAD:
                return [(1, (k + 1) % 3, s + AHEAD)] if nxt else []
            return [(2, (k + 2) % 3, s - (STEPS - AHEAD))] if nxt2 else []

        @block.sync
        def _(sp):
            def max_rows(n, k):
                sp.wait_ge(m_copied, n + 1)
                sp.sem_inc(env.sp_passed, 1)
                for i in range(3):
                    sp.dma_start(qs[k][MAXROW + i:MAXROW + i + 1, :, :].rearrange("p j t -> p (j t)"),
                                 mt[HG * TB * i:HG * TB * (i + 1), :]).then_inc(max_ready, 16)

            load_group(sp, env, 1, 1)
            sp.wait_ge(env.stored[1], STORES)
            for q in range(RAW_RING):
                split_load(sp, weights, q)
            max_rows(0, 0)

            def stage(r, k, nxt, nxt2):
                n = r * 3 + k
                if nxt2:
                    sp.wait_ge(st_done, ONE + n * 2 * STEPS)
                    sp.sem_inc(env.sp_passed, 1)
                    load_group(sp, env, n + 2, (k + 2) % 3)
                if nxt:
                    max_rows(n + 1, (k + 1) % 3)
            stages(sp, stage)
            split_sync(sp, env, weights)

        @block.gpsimd
        def _(pool):
            def copy_v(n, k):
                pool.tensor_copy(vg[k][:, :, :, 0:HD],
                                 env.vn[:, bass.ds(n, 1), :, :].rearrange("p o t (j d) -> p (o t) j d", j=HG)
                                 ).then_inc(v_ready, 1)

            copy_v(0, 0)

            def stage(r, k, nxt, nxt2):
                n = r * 3 + k
                if nxt2:
                    pool.wait_ge(st_done, ONE + n * 2 * STEPS)
                    pool.wait_ge(v_ready, n + 1)
                    pool.sem_inc(env.pool_passed, 1)
                    pool.memset(qs[(k + 2) % 3][MAXROW:MAXROW + 3, :, :].bitcast(U32), 0).then_inc(cleared, 1)
                    pool.wait_ge(cleared, n + 1)
                if nxt:
                    pool.wait_ge(pv_done, ONE + n * STEPS)
                    pool.sem_inc(env.pool_passed, 1)
                    copy_v(n + 1, (k + 1) % 3)
            stages(pool, stage)
            split_gpsimd(pool, weights)

        @block.tensor
        def _(pe):
            def score(n, k, blk, part):
                i = 4 * blk + part
                j, qt, h = i // 2 // TB, i // 2 % TB, i % 2
                pe.wait_ge(red_done, n * NS + i + 1)
                if i == TURN_TILE and not (isinstance(n, int) and n == 0):
                    pe.wait_ge(m_copied, n)
                pe.matmul(sc_bank(k, i)[:, :], qs[k][:, j, qt * P:(qt + 1) * P], ks[k][:, j, h * CH:(h + 1) * CH],
                          start=True, stop=True).then_inc(sc_done, 1)

            def transposed(n, k, s, pr):
                qh, kc = s // TB, s % TB
                pe.wait_ge(exp_done, n * 2 * STEPS + 2 * s + pr + 1)
                for h in range(2):
                    j = 2 * pr + h
                    mm = pe.matmul(st[pr][:, h, :], ks[k][:, j, kc * P:(kc + 1) * P],
                                   qs[k][:, j, qh * CH:(qh + 1) * CH], start=True, stop=True)
                mm.then_inc(st_done, 1)

            def weigh(n, k, s):
                qh, kc = s // TB, s % TB
                pe.wait_ge(exp_done, FREE + n * 2 * STEPS + 2 * s + 2)
                if kc == 0:
                    pe.wait_ge(u_out, ONE + n * 2 + qh)
                for j in range(HG):
                    mm = pe.matmul(pv[32 * j:32 * j + 32, :], vg[k][:, kc, j, :],
                                   prob[(2 * s + j // 2) % 4][:, j % 2, :], start=kc == 0, stop=kc == TB - 1)
                mm.then_inc(pv_done, 1)

            def turn_max(n, k, more):
                pe.wait_ge(m_step, 5 * n + 5)
                if more:
                    pe.wait_ge(red_done, (n + 1) * NS + TURN_TILE + 1)
                pe.transpose(turn_bank(k), mparts[:, :, :].rearrange("p a m -> p (a m)"),
                             env.ident16[:, :]).then_inc(turned, 1)

            pe.sem_inc(st_done, ONE)
            pe.sem_inc(pv_done, ONE)
            for n in range(2):
                pe.wait_ge(loaded[n], LOADS)
                for blk in range(STEPS if n == 0 else AHEAD):
                    if n == 1 and 4 * blk == TURN_TILE:
                        turn_max(0, 0, True)
                    for part in range(4):
                        score(n, n, blk, part)
            pe.wait_ge(max_ready, 48)
            transposed(0, 0, 0, 0)
            transposed(0, 0, 0, 1)

            def stage(r, k, nxt, nxt2):
                n = r * 3 + k
                pe.wait_ge(v_ready, n + 1)
                for s in range(STEPS):
                    if s == STEPS - AHEAD and nxt2:
                        pe.wait_ge(loaded[(k + 2) % 3], (r + (k + 2) // 3) * LOADS + LOADS)
                        pe.wait_ge(cleared, n + 1)
                    if s == STEPS - 1 and nxt:
                        pe.wait_ge(max_ready, 48 * n + 96)
                    blocks = score_blocks(s, k, nxt, nxt2)
                    for part in range(4):
                        for off, kk, blk in blocks:
                            score(n + off, kk, blk, part)
                        if part < 2:
                            if s < STEPS - 1:
                                transposed(n, k, s + 1, part)
                            elif nxt:
                                transposed(n + 1, (k + 1) % 3, 0, part)
                        if part == 2:
                            weigh(n, k, s)
                    if s == STEPS - AHEAD + TURN_TILE // 4 - 1 and nxt:
                        turn_max(n + 1, (k + 1) % 3, nxt2)
            stages(pe, stage)

        @block.scalar
        def _(act):
            act.sem_inc(exp_done, FREE)

            def copy_max(n, k):
                act.wait_ge(turned, n + 1)
                if not (isinstance(n, int) and n == 0):
                    act.wait_ge(max_ready, n * 48)
                act.copy(mt[:, :], turn_bank(k)).then_inc(m_copied, 1)

            def exponential(n, s, pr):
                e = 2 * s + pr
                act.wait_ge(st_done, ONE + n * 2 * STEPS + e + 1)
                act.activation(prob[e % 4][:, :, :].rearrange("p a c -> p (a c)"),
                               st[pr][:, :, :].rearrange("p a c -> p (a c)"), ACT.Exp,
                               scale=SCALE).then_inc(exp_done, 1)

            def sums_out(n, half):
                act.wait_ge(pv_done, ONE + n * STEPS + TB * (half + 1))
                act.copy(env.u[:, bass.ds(n, 1), half * CH:(half + 1) * CH].rearrange("p o c -> p (o c)"),
                         pv[:, :]).then_inc(u_out, 1)

            act.sem_inc(u_out, ONE)
            copy_max(0, 0)
            for pr in range(2):
                exponential(0, 0, pr)

            def stage(r, k, nxt, nxt2):
                n = r * 3 + k
                for s in range(STEPS):
                    act.wait_ge(pv_done, ONE + n * STEPS + s)
                    if s == TB:
                        sums_out(n, 0)
                    for pr in range(2):
                        if s < STEPS - 1:
                            exponential(n, s + 1, pr)
                        elif nxt:
                            exponential(n + 1, 0, pr)
                        if s == STEPS - 1 and pr == 1:
                            sums_out(n, 1)
                    if s == STEPS - AHEAD + TURN_TILE // 4 - 1 and nxt:
                        copy_max(n + 1, (k + 1) % 3)
            stages(act, stage)

        @block.vector
        def _(dve):
            dve.sem_inc(red_done, FREE_SC)

            def reduce_block(n, k, blk):
                for i in range(4 * blk, 4 * blk + 4):
                    dve.wait_ge(sc_done, n * NS + i + 1)
                    dve.tensor_reduce(mx[k][:, i // 2, i % 2:i % 2 + 1], sc_bank(k, i)[:, :], AX.X, ALU.max).then_inc(red_done, 1)

            def cut_max(n, k):
                dve.wait_ge(red_done, FREE_SC + (n + 1) * NS)
                dve.tensor_reduce(m1[:, :], mx[k][:, :, :], AX.X, ALU.max, negate=True).then_inc(m_step, 1)
                if not (isinstance(n, int) and n == 0):
                    dve.wait_ge(turned, n)
                dve.wait_ge(m_step, 5 * n + 1)
                dve.tensor_copy(mparts[:, 0, :], m1[:, :]).then_inc(m_step, 1)
                dve.wait_ge(m_step, 5 * n + 2)
                dve.tensor_tensor(m2[:, :], m1[:, :], mparts[:, 0, :], ALU.subtract).then_inc(m_step, 1)
                dve.wait_ge(m_step, 5 * n + 3)
                dve.tensor_copy(mparts[:, 1, :], m2[:, :]).then_inc(m_step, 1)
                dve.wait_ge(m_step, 5 * n + 4)
                dve.tensor_tensor(mparts[:, 2, :], m2[:, :], mparts[:, 1, :], ALU.subtract).then_inc(m_step, 1)

            for blk in range(STEPS):
                reduce_block(0, 0, blk)
            cut_max(0, 0)
            for blk in range(AHEAD):
                reduce_block(1, 1, blk)

            def stage(r, k, nxt, nxt2):
                n = r * 3 + k
                for s in range(STEPS):
                    for off, kk, blk in score_blocks(s, k, nxt, nxt2):
                        reduce_block(n + off, kk, blk)
                        if blk == STEPS - 1:
                            cut_max(n + off, kk)
            stages(dve, stage)
            split_vector(dve, env, weights)


def attend_banded(nc, env, tag):
    STEPS = TB
    FREE_ST, FREE_SC = 3, 2
    ONE = 1
    AHEAD = 4
    TURN = 0
    W2 = 2 * BAND
    with ExitStack() as ctx:
        sb = lambda n, s, d: ctx.enter_context(nc.sbuf_tensor(f"{tag}_{n}", s, d))
        ps = lambda n, s, d: ctx.enter_context(nc.psum_tensor(f"{tag}_{n}", s, d))
        sem = lambda n: semaphore(nc, env, f"{tag}_{n}")
        qs, ks, vg, loaded = env.qs, env.ks, env.vg, env.loaded
        prob = [sb(f"prob{i}", [P, W2], F32) for i in range(4)]
        m1 = [sb(f"m1{i}", [P, HG, TB], F32) for i in range(3)]
        m2 = sb("m2", [P, HG * TB], F32)
        mparts = sb("mparts", [P, 3, HG * TB], BF16)
        mt = sb("mt", [3 * HG * TB, P], BF16)
        sc = [ps(f"sc{i}", [P, W2], F32) for i in range(2)]
        st = [ps(f"st{i}", [P, W2], F32) for i in range(3)]
        pv = [ps(f"pv{i}", [P, CH], F32) for i in range(2)]
        turn = ps("turn", [P, 2 * CH], BF16)
        (cleared, v_ready, sc_done, red_done, m_step, turned, m_copied, max_ready,
         st_done, exp_done, pv_done, u_out) = map(sem, (
            "cleared", "v_ready", "sc_done", "red_done", "m_step", "turned", "m_copied",
            "max_ready", "st_done", "exp_done", "pv_done", "u_out"))
        block = ctx.enter_context(nc.Block())
        mask_q, mask_q0, mask_k = env.masks

        LOOPED = 6

        def stages(eng, stage):
            with eng.Fori(0, LOOPED // 3) as i:
                for k in range(3):
                    stage(i, k, True, True)
            stage(LOOPED // 3, 0, True, False)
            stage(LOOPED // 3, 1, False, False)

        def score_blocks(s, k, nxt, nxt2):
            if s < STEPS - AHEAD:
                return [(1, (k + 1) % 3, s + AHEAD)] if nxt else []
            return [(2, (k + 2) % 3, s - (STEPS - AHEAD))] if nxt2 else []

        @block.sync
        def _(sp):
            def max_rows(n, k):
                sp.wait_ge(m_copied, n + 1)
                sp.sem_inc(env.sp_passed, 1)
                for i in range(3):
                    sp.dma_start(qs[k][MAXROW + i:MAXROW + i + 1, :, :].rearrange("p j t -> p (j t)"),
                                 mt[HG * TB * i:HG * TB * (i + 1), :]).then_inc(max_ready, 16)

            load_group(sp, env, 1, 1)
            max_rows(0, 0)
            sp.wait_ge(env.stored[1], STORES)

            def stage(r, k, nxt, nxt2):
                n = r * 3 + k
                if nxt2:
                    sp.wait_ge(st_done, ONE + n * 2 * STEPS)
                    sp.sem_inc(env.sp_passed, 1)
                    load_group(sp, env, n + 2, (k + 2) % 3)
                if nxt:
                    max_rows(n + 1, (k + 1) % 3)
            stages(sp, stage)

        @block.gpsimd
        def _(pool):
            def copy_v(n, k):
                pool.tensor_copy(vg[k][:, :, :, 0:HD],
                                 env.vn[:, bass.ds(n, 1), :, :].rearrange("p o t (j d) -> p (o t) j d", j=HG)
                                 ).then_inc(v_ready, 1)

            copy_v(0, 0)

            def stage(r, k, nxt, nxt2):
                n = r * 3 + k
                if nxt2:
                    pool.wait_ge(st_done, ONE + n * 2 * STEPS)
                    pool.wait_ge(v_ready, n + 1)
                    pool.sem_inc(env.pool_passed, 1)
                    pool.memset(qs[(k + 2) % 3][MAXROW:MAXROW + 3, :, :].bitcast(U32), 0).then_inc(cleared, 1)
                    pool.wait_ge(cleared, n + 1)
                if nxt:
                    pool.wait_ge(pv_done, ONE + n * STEPS)
                    pool.sem_inc(env.pool_passed, 1)
                    copy_v(n + 1, (k + 1) % 3)
            stages(pool, stage)

        @block.tensor
        def _(pe):
            def scores(n, k, qt):
                mask = mask_q if qt else mask_q0
                for pr in range(2):
                    pe.wait_ge(red_done, n * 2 * STEPS + 2 * qt + pr + 1)
                    pe.matmul(sc[pr][:, :], env.ident16[:, :], mask[:, :], start=True, stop=True)
                    for h in range(2):
                        j = 2 * pr + h
                        first = 0 if qt else WIN
                        mm = pe.matmul(sc[pr][:, h * BAND + first:(h + 1) * BAND], qs[k][:, j, qt * P:(qt + 1) * P],
                                       ks[k][:, j, qt * P - WIN + first:(qt + 1) * P], start=False, stop=True,
                                           skip_group_check=True)
                    mm.then_inc(sc_done, 1)

            def weigh(n, k, s):
                pe.wait_ge(exp_done, FREE_ST + n * 2 * STEPS + 2 * s + 2)
                if s == 0:
                    pe.wait_ge(u_out, ONE + n * 2)
                spans = {3: ((0, P), (P, BAND)), 7: ((0, P),)}.get(s, ((0, BAND),))
                for a, b in spans:
                    q0 = s * P + a
                    for j in range(HG):
                        mm = pe.matmul(pv[q0 // CH][32 * j:32 * j + 32, q0 % CH:q0 % CH + b - a], vg[k][:, s, j, :],
                                       prob[(2 * s + j // 2) % 4][:, (j % 2) * BAND + a:(j % 2) * BAND + b],
                                       start=s == 0 or (s == 3 and a > 0), stop=True,
                                       skip_group_check=True)
                mm.then_inc(pv_done, 1)

            def turn_max(n):
                pe.wait_ge(m_step, 4 * n + 4)
                pe.transpose(turn[0:3 * HG * TB, 0:P], mparts[:, :, :].rearrange("p a m -> p (a m)"),
                             env.ident16[:, :]).then_inc(turned, 1)

            pe.sem_inc(st_done, ONE)
            pe.sem_inc(pv_done, ONE)
            for n in range(2):
                pe.wait_ge(loaded[n], LOADS)
                for qt in range(STEPS if n == 0 else AHEAD):
                    scores(n, n, qt)
                if n == 0:
                    turn_max(0)

            def stage(r, k, nxt, nxt2):
                n = r * 3 + k
                pe.wait_ge(max_ready, 48 * n + 48)
                pe.wait_ge(v_ready, n + 1)
                for s in range(STEPS):
                    width = BAND if s < STEPS - 1 else P
                    if s == STEPS - AHEAD and nxt2:
                        pe.wait_ge(loaded[(k + 2) % 3], (r + (k + 2) // 3) * LOADS + LOADS)
                        pe.wait_ge(cleared, n + 1)
                    for pr in range(2):
                        e = 2 * s + pr
                        bank = st[(k + e) % 3]
                        pe.wait_ge(exp_done, n * 2 * STEPS + e + 1)
                        pe.matmul(bank[:, :], env.ident16[:, :], mask_k[:, :], start=True, stop=True)
                        for h in range(2):
                            j = 2 * pr + h
                            mm = pe.matmul(bank[:, h * BAND:h * BAND + width], ks[k][:, j, s * P:(s + 1) * P],
                                           qs[k][:, j, s * P:s * P + width], start=False, stop=True,
                                           skip_group_check=True)
                        mm.then_inc(st_done, 1)
                    for off, kk, qt in score_blocks(s, k, nxt, nxt2):
                        scores(n + off, kk, qt)
                    if s:
                        weigh(n, k, s - 1)
                    if s == STEPS - AHEAD + TURN and nxt:
                        turn_max(n + 1)
                weigh(n, k, STEPS - 1)
            stages(pe, stage)

        @block.scalar
        def _(act):
            act.sem_inc(exp_done, FREE_ST)
            act.sem_inc(u_out, ONE)

            def copy_max(n):
                act.wait_ge(turned, n + 1)
                if not (isinstance(n, int) and n == 0):
                    act.wait_ge(max_ready, n * 48)
                act.copy(mt[:, :], turn[0:3 * HG * TB, 0:P]).then_inc(m_copied, 1)

            copy_max(0)

            def stage(r, k, nxt, nxt2):
                n = r * 3 + k
                for s in range(STEPS):
                    if s >= 2:
                        act.wait_ge(pv_done, ONE + n * STEPS + s - 1)
                    for pr in range(2):
                        e = 2 * s + pr
                        act.wait_ge(st_done, ONE + n * 2 * STEPS + e + 1)
                        act.activation(prob[e % 4][:, :], st[(k + e) % 3][:, :], ACT.Exp,
                                       scale=SCALE).then_inc(exp_done, 1)
                    if s in (TB // 2, STEPS - 1):
                        half = 0 if s == TB // 2 else 1
                        act.wait_ge(pv_done, ONE + n * STEPS + TB // 2 * (half + 1))
                        act.copy(env.u[:, bass.ds(n, 1), half * CH:(half + 1) * CH].rearrange("p o c -> p (o c)"),
                                 pv[half][:, :]).then_inc(u_out, 1)
                    if s == STEPS - AHEAD + TURN and nxt:
                        copy_max(n + 1)
            stages(act, stage)

        @block.vector
        def _(dve):
            dve.sem_inc(red_done, FREE_SC)

            def reduce_tile(n, k, qt):
                for pr in range(2):
                    dve.wait_ge(sc_done, n * 2 * STEPS + 2 * qt + pr + 1)
                    dve.tensor_reduce(m1[k][:, 2 * pr:2 * pr + 2, qt], sc[pr][:, :].rearrange("p (h r) -> p h r", h=2),
                                      AX.X, ALU.max, negate=True).then_inc(red_done, 1)

            def cut_max(n, k):
                m = m1[k][:, :, :].rearrange("p j t -> p (j t)")
                dve.wait_ge(red_done, FREE_SC + (n + 1) * 2 * STEPS)
                if not (isinstance(n, int) and n == 0):
                    dve.wait_ge(turned, n)
                dve.tensor_copy(mparts[:, 0, :], m).then_inc(m_step, 1)
                dve.wait_ge(m_step, 4 * n + 1)
                dve.tensor_tensor(m2[:, :], m, mparts[:, 0, :], ALU.subtract).then_inc(m_step, 1)
                dve.wait_ge(m_step, 4 * n + 2)
                dve.tensor_copy(mparts[:, 1, :], m2[:, :]).then_inc(m_step, 1)
                dve.wait_ge(m_step, 4 * n + 3)
                dve.tensor_tensor(mparts[:, 2, :], m2[:, :], mparts[:, 1, :], ALU.subtract).then_inc(m_step, 1)

            for qt in range(STEPS):
                reduce_tile(0, 0, qt)
            cut_max(0, 0)
            for qt in range(AHEAD):
                reduce_tile(1, 1, qt)

            def stage(r, k, nxt, nxt2):
                n = r * 3 + k
                for s in range(STEPS):
                    for off, kk, qt in score_blocks(s, k, nxt, nxt2):
                        reduce_tile(n + off, kk, qt)
                        if qt == STEPS - 1:
                            cut_max(n + off, kk)
            stages(dve, stage)


def project_out(nc, env, tag):
    with ExitStack() as ctx:
        sb = lambda n, s, d: ctx.enter_context(nc.sbuf_tensor(f"{tag}_{n}", s, d))
        ps = lambda n, s, d: ctx.enter_context(nc.psum_tensor(f"{tag}_{n}", s, d))
        sem = lambda n: semaphore(nc, env, f"{tag}_{n}")
        rden = sb("rden", [P, NT, H], F32)
        att = sb("att", [P, 2, C], F32)
        attT = sb("attT", [P, 2, C], F32)
        xb = sb("xb", [P, NT, C], F32)
        ut = [ps(f"ut{i}", [P, CH], F32) for i in range(3)]
        at = [ps(f"at{i}", [P, P], F32) for i in range(2)]
        out = [ps(f"out{i}", [P, C], F32) for i in range(2)]
        ut_done, rden_ready, att_ready, at_done, attT_ready, out_done, xb_ready, x_ready = map(sem, (
            "ut_done", "rden_ready", "att_ready", "at_done", "attT_ready", "out_done", "xb_ready", "x_ready"))
        block = ctx.enter_context(nc.Block())

        @block.tensor
        def _(pe):
            def turn(t):
                if t >= 3:
                    pe.wait_ge(att_ready, t - 2)
                for g in range(G):
                    mm = pe.transpose(ut[t % 3][:, g * P:(g + 1) * P],
                                      env.u[:, G * (t // TB) + g, (t % TB) * P:(t % TB + 1) * P], env.ident[:, :])
                mm.then_inc(ut_done, 1)

            def turn_back(t):
                pe.wait_ge(att_ready, t + 1)
                if t >= 2:
                    pe.wait_ge(attT_ready, t - 1)
                pe.transpose(at[t % 2][:, :], att[:, t % 2, :], env.ident[:, :]).then_inc(at_done, 1)

            def project(t):
                pe.wait_ge(attT_ready, t + 1)
                if t >= 2:
                    pe.wait_ge(x_ready, t - 1)
                pe.matmul(out[t % 2][:, :], attT[:, t % 2, :], env.wo[:, :], start=True, stop=True).then_inc(out_done, 1)

            turn(0)
            turn(1)
            for t in range(NT):
                if t + 2 < NT:
                    turn(t + 2)
                turn_back(t)
                if t:
                    project(t - 1)
            project(NT - 1)

        @block.scalar
        def _(act):
            for t in range(NT):
                act.wait_ge(at_done, t + 1)
                if t >= 2:
                    act.wait_ge(out_done, t - 1)
                act.copy(attT[:, t % 2, :], at[t % 2][:, :]).then_inc(attT_ready, 1)

        @block.vector
        def _(dve):
            dve.tensor_tensor(xb[:, :, :], env.x[:, :, :],
                              env.bo[:, :].rearrange("p (a c) -> p a c", a=1).to_broadcast([P, NT, C]),
                              ALU.add).then_inc(xb_ready, 1)
            dve.wait_ge(xb_ready, 1)

            def divide(t):
                heads = ut[t % 3][:, :].rearrange("p (h i) -> p h i", h=H)
                dve.wait_ge(ut_done, t + 1)
                dve.reciprocal(rden[:, t, :], heads[:, :, HD]).then_inc(rden_ready, 1)
                dve.wait_ge(rden_ready, t + 1)
                if t >= 2:
                    dve.wait_ge(at_done, t - 1)
                dve.tensor_tensor(att[:, t % 2, :].rearrange("p (h i) -> p h i", h=H), heads[:, :, 0:HD],
                                  rden[:, t, :].rearrange("p (h i) -> p h i", i=1).to_broadcast([P, H, HD]),
                                  ALU.mult).then_inc(att_ready, 1)

            def add(t):
                dve.wait_ge(out_done, t + 1)
                dve.tensor_tensor(env.x[:, t, :], out[t % 2][:, :], xb[:, t, :], ALU.add).then_inc(x_ready, 1)

            for t in range(NT):
                divide(t)
                if t >= 2:
                    add(t - 2)
            add(NT - 2)
            add(NT - 1)


ZERO_ROWS = [(k, 64, P) for k in range(3)] + [(k, 32, MAXROW) for k in range(6)]


def set_up(nc, env, d):
    with ExitStack() as ctx:
        sem = lambda n: semaphore(nc, env, f"setup_{n}")
        loaded, made, rows_set = map(sem, ("loaded", "made", "rows_set"))
        block = ctx.enter_context(nc.Block())

        @block.sync
        def _(sp):
            n = 0
            for c in range(NC):
                sp.dma_start(env.x[:, 4 * c:4 * c + 4, :], d["x"].rearrange("b s c -> (b s) c").rearrange(
                    "(t p) c -> p t c", p=P)[:, 4 * c:4 * c + 4, :]).then_inc(loaded, 16)
                n += 1
            for a in (env.a, env.b):
                for dst, src in ((a.wqk[:, :, :], d[a.tag + "wqk"]), (a.wv[:, :], d[a.tag + "wv"]),
                                 (a.wo[:, :], d[a.tag + "wo"]),
                                 (a.bqk[:, :], d[a.tag + "bqk"]),
                                 (a.bv[:, :], d[a.tag + "bv"].rearrange("(o c) -> o c", o=1).to_broadcast([P, C])),
                                 (a.bo[:, :], d[a.tag + "bo"].rearrange("(o c) -> o c", o=1).to_broadcast([P, C]))):
                    sp.dma_start(dst, src).then_inc(loaded, 16)
                    n += 1
            for dst, src in ((env.gate[:, :], d["gate"]), (env.gate_bias[:, :], d["gate_bias"].rearrange(
                    "(o c) -> o c", o=1).to_broadcast([P, 64]))):
                sp.dma_start(dst, src).then_inc(loaded, 16)
                n += 1
            sp.wait_ge(loaded, 16 * n)

        @block.vector
        def _(dve):
            for t, a, b in ZERO_ROWS[:4]:
                dve.memset(env.stacks[t][a:b, :, :].bitcast(U32), 0).then_inc(rows_set, 1)
            dve.wait_ge(rows_set, 4)

        @block.gpsimd
        def _(pool):
            for m in (env.ident[:, :], env.ident16[:, :], *(m[:, :] for m in env.masks)):
                pool.memset(m, 0.0).then_inc(made, 1)
            pool.wait_ge(made, 2 + len(env.masks))
            for m in (env.ident, env.ident16):
                pool.affine_select(out=m[:, :], in_=m[:, :], compare_op=ALU.not_equal, fill=1.0, base=0,
                                   pattern=[[-1, P]], channel_multiplier=1).then_inc(made, 1)
            pool.wait_ge(made, 7)

            def keep(m, base, step, multiplier):
                v = m[:, :].rearrange("p (a r) -> p a r", a=2)
                pool.affine_select(out=v, in_=v, compare_op=ALU.is_ge, fill=BARRED, base=base,
                                   pattern=[[0, 2], [step, BAND]], channel_multiplier=multiplier).then_inc(made, 1)

            mq, mq0, mk = env.masks
            for m in (mq, mq0):
                keep(m, -1, 1, -1)
            keep(mk, 0, 1, -1)
            pool.wait_ge(made, 10)
            for m in (mq, mq0):
                keep(m, WIN, -1, 1)
            keep(mk, WIN - 1, -1, 1)
            pool.wait_ge(made, 13)
            keep(mq0, -WIN, 1, 0)
            pool.wait_ge(made, 14)
            for m in (env.fresh, env.fresh_groups):
                pool.memset(m[:, :, :], 1.0).then_inc(made, 1)
            pool.wait_ge(made, 16)
            for m in (env.fresh, env.fresh_groups):
                pool.memset(m[:, :, 0:1], 0.0).then_inc(made, 1)
            pool.wait_ge(made, 18)


def attention(nc, env, a, tag, attend, first=False):
    env.wqk, env.bqk, env.wv, env.bv, env.wo, env.bo = a.wqk, a.bqk, a.wv, a.bv, a.wo, a.bo
    with ExitStack() as ctx:
        sb = lambda n, s, d: ctx.enter_context(nc.sbuf_tensor(f"{tag}_{n}", s, d))
        env.u = sb("u", [P, NG, S], F32)
        env.loaded = [semaphore(nc, env, f"{tag}_loaded{i}") for i in range(3)]
        env.stored = [semaphore(nc, env, f"{tag}_stored{b}") for b in range(B)]
        env.q_cleared = semaphore(nc, env, f"{tag}_q_cleared")
        env.vn = sb("vn", [P, NG, TB, HG * HD], F32)
        with ExitStack() as c2:
            env.xnT = c2.enter_context(nc.sbuf_tensor(f"{tag}_xnT", [P, B * S], F32))
            project_qkv(nc, env, tag + "qkv", first)
        attend(nc, env, tag + "att")
        project_out(nc, env, tag + "out")
    end_of_layer(nc, env)


E, INTER, GROUPS, TOPG, TOPK = 64, 64, 8, 4, 6
SHARED = 2
PAIRS = (E + SHARED) // 2
ROWS = SHARED + E
ALL = PAIRS * P
EXP_BITS = 0x7F800000
HALF_TOP = 2.0 ** 14


PIECE = 11
PIECES = [(i, j) for i in range(3) for j in range(0, PAIRS, PIECE)]
RAW_RING, CUT_RING = 4, 3
POOL_PIECES = (1, 4, 7)


def splitter(nc, ctx, env, d):
    sb = lambda n, s, t: ctx.enter_context(nc.sbuf_tensor(f"split_{n}", s, t))
    sem = lambda n: semaphore(nc, env, f"split_{n}")
    w = Env()
    w.raw = [sb(f"raw{i}", [P, PIECE, P], F32) for i in range(RAW_RING)]
    w.cut = [sb(f"cut{i}", [P, PIECE, 2, P], F16) for i in range(CUT_RING)]
    w.top = sb("top", [P, len(PIECES)], F32)
    w.alltop = sb("alltop", [P, len(PIECES)], F32)
    w.pow2 = sb("pow2", [P, 3], F32)
    w.scale = sb("scale", [P, 3], F32)
    w.raw_in = [sem(f"raw_in{i}") for i in range(RAW_RING)]
    w.stored = [sem(f"stored{i}") for i in range(CUT_RING)]
    w.topped, w.reduced, w.step, w.high, w.pool_high, w.low = map(sem, (
        "topped", "reduced", "step", "high", "pool_high", "low"))
    w.sources = [d[n].rearrange("p (j c) -> p j c", c=P) for n in ("wg", "wu", "wd")]
    return w


def split_load(sp, w, q):
    i, j = PIECES[q % len(PIECES)]
    sp.dma_start(w.raw[q % RAW_RING][:, :, :], w.sources[i][:, j:j + PIECE, :]).then_inc(w.raw_in[q % RAW_RING], 16)


def split_sync(sp, env, w):
    N = len(PIECES)

    def store(p):
        i, j = PIECES[p]
        sp.wait_ge(w.low, p + 1)
        sp.dma_start(env.wsplit[j:j + PIECE, :, 2 * i * P:2 * (i + 1) * P].rearrange("j p n -> p j n"),
                     w.cut[p % CUT_RING][:, :, :, :].rearrange("p j a c -> p j (a c)")).then_inc(w.stored[p % CUT_RING], 16)

    for q in range(RAW_RING, 2 * N):
        before = q - RAW_RING
        if before < N:
            sp.wait_ge(w.topped, before + 1)
        else:
            sp.wait_ge(w.low, before - N + 1)
        split_load(sp, w, q)
        if q - N >= RAW_RING - 1:
            store(q - N - (RAW_RING - 1))
    for p in range(N - RAW_RING + 1, N):
        store(p)
    for i in range(CUT_RING):
        sp.wait_ge(w.stored[i], 16 * (N // CUT_RING))


def split_gpsimd(pool, w):
    N = len(PIECES)
    pool.wait_ge(w.topped, N)
    pool.partition_all_reduce(w.alltop[:, :], w.top[:, :], P, bass.bass_isa.ReduceOp.max).then_inc(w.reduced, 1)
    pool.wait_ge(w.step, 4)
    for n, p in enumerate(POOL_PIECES):
        i, q = PIECES[p][0], N + p
        pool.wait_ge(w.raw_in[q % RAW_RING], 16 * (q // RAW_RING + 1))
        if p >= CUT_RING:
            pool.wait_ge(w.stored[p % CUT_RING], 16 * (p // CUT_RING))
        pool.tensor_scalar(w.cut[p % CUT_RING][:, :, 0, :], w.raw[q % RAW_RING][:, :, :], w.scale[:, i:i + 1], None,
                           ALU.mult).then_inc(w.pool_high, 1)


def split_vector(dve, env, w):
    N = len(PIECES)
    for q in range(N):
        dve.wait_ge(w.raw_in[q % RAW_RING], 16 * (q // RAW_RING + 1))
        dve.tensor_reduce(w.top[:, q:q + 1], w.raw[q % RAW_RING][:, :, :].rearrange("p j c -> p (j c)"), AX.X, ALU.max,
                          apply_absolute_value=True).then_inc(w.topped, 1)
    dve.wait_ge(w.reduced, 1)
    dve.tensor_reduce(w.pow2[:, :], w.alltop[:, :].rearrange("p (i j) -> p i j", i=3), AX.X, ALU.max).then_inc(w.step, 1)
    dve.wait_ge(w.step, 1)
    dve.tensor_scalar(w.pow2[:, :].bitcast(I32), w.pow2[:, :].bitcast(I32), EXP_BITS, None,
                      ALU.bitwise_and).then_inc(w.step, 1)
    dve.wait_ge(w.step, 2)
    dve.tensor_scalar(w.pow2[:, :], w.pow2[:, :], 2.0 ** -60, 1.0 / HALF_TOP, ALU.max, ALU.mult).then_inc(w.step, 1)
    dve.wait_ge(w.step, 3)
    dve.reciprocal(w.scale[:, :], w.pow2[:, :]).then_inc(w.step, 1)
    dve.tensor_copy(env.unscale[:, 0:3], w.pow2[:, :]).then_inc(w.step, 1)
    dve.wait_ge(w.step, 5)
    dve.tensor_tensor(env.unscale[:, 3:4], w.scale[:, 0:1], w.scale[:, 1:2], ALU.mult).then_inc(w.step, 1)
    dve.wait_ge(w.step, 6)
    dve.tensor_scalar(env.unscale[:, 3:4], env.unscale[:, 3:4], 2.0 ** -29, None, ALU.mult).then_inc(w.step, 1)
    dve.tensor_scalar(env.unscale[:, 4:5], env.unscale[:, 0:1], env.unscale[:, 1:2], 2.0 ** 29,
                      ALU.mult, ALU.mult).then_inc(w.step, 1)
    dve.wait_ge(w.step, 8)
    dve.tensor_tensor(env.unscale[:, 4:5], env.unscale[:, 4:5], env.unscale[:, 2:3], ALU.mult).then_inc(w.step, 1)
    done = 0
    for p, (i, j) in enumerate(PIECES):
        q = N + p
        if p in POOL_PIECES:
            dve.wait_ge(w.pool_high, POOL_PIECES.index(p) + 1)
        else:
            dve.wait_ge(w.raw_in[q % RAW_RING], 16 * (q // RAW_RING + 1))
            if p >= CUT_RING:
                dve.wait_ge(w.stored[p % CUT_RING], 16 * (p // CUT_RING))
            dve.tensor_scalar(w.cut[p % CUT_RING][:, :, 0, :], w.raw[q % RAW_RING][:, :, :], w.scale[:, i:i + 1], None,
                              ALU.mult).then_inc(w.high, 1)
            done += 1
            dve.wait_ge(w.high, done)
        dve.scalar_tensor_tensor(w.cut[p % CUT_RING][:, :, 1, :], w.raw[q % RAW_RING][:, :, :], w.scale[:, i:i + 1],
                                 w.cut[p % CUT_RING][:, :, 0, :], ALU.mult, ALU.subtract).then_inc(w.low, 1)
    dve.wait_ge(w.step, 9)


def route(nc, env, tag):
    with ExitStack() as ctx:
        sb = lambda n, s, t: ctx.enter_context(nc.sbuf_tensor(f"{tag}_{n}", s, t))
        ps = lambda n, s, t: ctx.enter_context(nc.psum_tensor(f"{tag}_{n}", s, t))
        sem = lambda n: semaphore(nc, env, f"{tag}_{n}")
        sc, masked, weighted = (sb(n, [P, NT, E], F32) for n in ("sc", "masked", "weighted"))
        gs = sb("gs", [P, NT, GROUPS], F32)
        gsel = sb("gsel", [P, NT, GROUPS], F32)
        total = sb("total", [P, NT], F32)
        inv = sb("inv", [P, NT], F32)
        lg = [ps(f"lg{i}", [P, NT // 2, E], F32) for i in range(2)]
        lg_done, sig_ready, step, masked_ready, inv_ready, weighted_ready = map(sem, (
            "lg_done", "sig_ready", "step", "masked_ready", "inv_ready", "weighted_ready"))
        xh_ready, xl_ready = map(sem, ("xh_ready", "xl_ready"))

        def picker(name, n):
            w = Env()
            w.top8 = sb(name + "_top8", [P, NT, 8], F32)
            w.above = sb(name + "_above", [P, NT, 8], F32)
            w.quota = sb(name + "_quota", [P, NT], F32)
            w.gt, w.eq, w.rank, w.keep = (sb(f"{name}_{m}", [P, NT, n], BF16) for m in ("gt", "eq", "rank", "keep"))
            return w
        of_groups, of_experts = picker("groups", GROUPS), picker("experts", E)
        norm = layer_norm(nc, ctx, env, tag + "ln")
        block = ctx.enter_context(nc.Block())

        @block.tensor
        def _(pe):
            norm_tensor(pe, env, norm)
            for t in range(NT):
                if t % 4 == 0:
                    pe.wait_ge(norm.copied, t // 4 + 1)
                mm = pe.matmul(lg[t // 8][:, t % 8, :], env.xnT[:, t * P:(t + 1) * P], env.gate[:, :],
                               start=True, stop=True)
                if t % 8 == 7:
                    mm.then_inc(lg_done, 1)

        @block.scalar
        def _(act):
            norm_scalar(act, env, norm)
            for i in range(2):
                act.wait_ge(lg_done, i + 1)
                act.activation(sc[:, 8 * i:8 * i + 8, :], lg[i][:, :, :], ACT.Sigmoid).then_inc(sig_ready, 1)
            for c in range(NC):
                cs = slice(c * CH, (c + 1) * CH)
                act.copy(env.xh[:, cs], env.xnT[:, cs]).then_inc(xh_ready, 1)

        @block.gpsimd
        def _(pool):
            for c in range(NC):
                cs = slice(c * CH, (c + 1) * CH)
                pool.wait_ge(xh_ready, c + 1)
                pool.tensor_tensor(env.xl[:, cs], env.xnT[:, cs], env.xh[:, cs], ALU.subtract).then_inc(xl_ready, 1)
            pool.wait_ge(xl_ready, NC)
            pool.wait_ge(inv_ready, 1)
            pool.tensor_tensor(weighted[:, :, :], masked[:, :, :],
                               inv[:, :].rearrange("p (t o) -> p t o", o=1).to_broadcast([P, NT, E]),
                               ALU.mult).then_inc(weighted_ready, 1)

        @block.sync
        def _(sp):
            for k in range(3):
                load_matrices(sp, env, k, k)

        @block.vector
        def _(dve):
            count = [0]

            def goes_on(ins):
                ins.then_inc(step, 1)
                count[0] += 1

            def done(ins):
                goes_on(ins)
                dve.wait_ge(step, count[0])

            def best(w, values):
                for t in range(NT):
                    goes_on(dve.max(w.top8[:, t, :], values[:, t, :]))
                dve.wait_ge(step, count[0])

            def pick(w, values, n, k, fresh):
                wide = lambda a, m: a.rearrange("p (t o) -> p t o", o=1).to_broadcast([P, NT, m])
                kth = w.top8[:, :, k - 1]
                goes_on(dve.tensor_tensor(w.above[:, :, 0:k], w.top8[:, :, 0:k], wide(kth, k), ALU.is_gt))
                goes_on(dve.tensor_tensor(w.gt[:, :, :], values[:, :, :], wide(kth, n), ALU.is_gt))
                done(dve.tensor_tensor(w.eq[:, :, :], values[:, :, :], wide(kth, n), ALU.is_equal))
                goes_on(dve.tensor_reduce(w.quota[:, :], w.above[:, :, 0:k], AX.X, ALU.add))
                flat = lambda a: a[:, :, :].rearrange("p t e -> p (t e)")
                done(dve.tensor_tensor_scan(flat(w.rank), flat(fresh), flat(w.eq), 0.0, ALU.mult, ALU.add))
                done(dve.tensor_scalar(w.quota[:, :], w.quota[:, :], -1.0, float(k), ALU.mult, ALU.add))
                done(dve.tensor_tensor(w.keep[:, :, :], w.rank[:, :, :], wide(w.quota[:, :], n), ALU.is_le))
                done(dve.tensor_tensor(w.keep[:, :, :], w.keep[:, :, :], w.eq[:, :, :], ALU.mult))
                done(dve.tensor_tensor(w.keep[:, :, :], w.keep[:, :, :], w.gt[:, :, :], ALU.add))

            norm_vector(dve, env, norm)
            dve.wait_ge(sig_ready, 2)
            done(dve.tensor_tensor(sc[:, :, :], sc[:, :, :], env.gate_bias[:, :].rearrange(
                "p (o e) -> p o e", o=1).to_broadcast([P, NT, E]), ALU.add))
            done(dve.tensor_reduce(gs[:, :, :], sc[:, :, :].rearrange("p t (g e) -> p t g e", g=GROUPS), AX.X, ALU.max))
            best(of_groups, gs)
            pick(of_groups, gs, GROUPS, TOPG, env.fresh_groups)
            square = lambda a: a[:, :, :].rearrange("p t (g o) -> p t g o", g=GROUPS)
            done(dve.tensor_copy(gsel[:, :, :], of_groups.keep[:, :, :]))
            dve.tensor_tensor(square(masked), square(sc), gsel[:, :, :].rearrange(
                "p t (g o) -> p t g o", o=1).to_broadcast([P, NT, GROUPS, GROUPS]), ALU.mult).then_inc(masked_ready, 1)
            dve.wait_ge(masked_ready, 1)
            best(of_experts, masked)
            done(dve.tensor_reduce(total[:, :], of_experts.top8[:, :, 0:TOPK], AX.X, ALU.add))
            done(dve.tensor_scalar(total[:, :], total[:, :], 1e-8, None, ALU.add))
            done(dve.reciprocal(inv[:, :], total[:, :]))
            dve.tensor_scalar(inv[:, :], inv[:, :], env.unscale[:, 3:4], None, ALU.mult).then_inc(inv_ready, 1)
            pick(of_experts, masked, E, TOPK, env.fresh)
            goes_on(dve.tensor_copy(env.comb[:, :, 0:SHARED], env.unscale[:, 3:4].rearrange("p (o e) -> p o e", o=1)
                                    .to_broadcast([P, NT, 2])))
            dve.wait_ge(weighted_ready, 1)
            done(dve.tensor_tensor(env.comb[:, :, SHARED:ROWS], of_experts.keep[:, :, :], weighted[:, :, :], ALU.mult))


def load_matrices(sp, env, j, k):
    sp.dma_start(env.wt[k][:, :, :].rearrange("p a c -> p (a c)"), env.wsplit[j, :, :]).then_inc(env.wt_in[k], 16)


def experts(nc, env, tag):
    QN = PAIRS * NC
    FREE_UP, FREE3 = 2, 3
    ONE = 1
    BODY = 3 * NC
    ROUNDS = PAIRS // 3
    with ExitStack() as ctx:
        sb = lambda n, s, t: ctx.enter_context(nc.sbuf_tensor(f"{tag}_{n}", s, t))
        ps = lambda n, s, t: ctx.enter_context(nc.psum_tensor(f"{tag}_{n}", s, t))
        sem = lambda n: semaphore(nc, env, f"{tag}_{n}")
        wt, wt_in = env.wt, env.wt_in
        combT = sb("combT", [ROWS, B * S], F32)
        cb = [sb(f"cb{i}", [P, B * S], F32) for i in range(3)]
        sil = [sb(f"sil{i}", [P, CH], F32) for i in range(2)]
        act_up = [sb(f"act_up{i}", [P, CH], F32) for i in range(3)]
        hid = [sb(f"hid{i}", [P, CH], F32) for i in range(3)]
        high = [sb(f"high{i}", [P, CH], F16) for i in range(3)]
        low = [sb(f"low{i}", [P, CH], F16) for i in range(3)]
        sums = [sb(f"sums{i}", [P, CH], F32) for i in range(NC)]
        gate = [ps(f"gate{i}", [P, CH], F32) for i in range(2)]
        up = [ps(f"up{i}", [P, CH], F32) for i in range(2)]
        acc = [ps(f"acc{i}", [P, CH], F32) for i in range(NC)]
        cb_in = [sem(f"cb_in{i}") for i in range(3)]
        g_done, u_done, sil_ready, up_ready, hid_ready, high_ready, low_ready, down_done = map(sem, (
            "g_done", "u_done", "sil_ready", "up_ready", "hid_ready", "high_ready", "low_ready", "down_done"))
        sum_ready, back_done, x_ready, comb_turned, comb_copied, comb_stored, cb_filled = map(sem, (
            "sum_ready", "back_done", "x_ready", "comb_turned", "comb_copied", "comb_stored", "cb_filled"))
        block = ctx.enter_context(nc.Block())

        def looped(eng, body):
            with eng.Fori(0, ROUNDS - 1) as r:
                for i in range(BODY):
                    body(r * BODY + i, i, r, False)
            for i in range(BODY):
                body((ROUNDS - 1) * BODY + i, i, ROUNDS - 1, True)

        @block.sync
        def _(sp):
            def weights(j, k):
                for e in range(2):
                    sp.dma_start(cb[k][64 * e:64 * e + 64, :],
                                 env.comb2[j, e:e + 1, :].to_broadcast([64, B * S])).then_inc(cb_in[k], 16)

            sp.sem_inc(cb_in[0], 32)
            for c in range(NC):
                sp.wait_ge(comb_copied, c + 1)
                sp.dma_start(env.comb_rows[:, c * CH:(c + 1) * CH], combT[:, c * CH:(c + 1) * CH]).then_inc(comb_stored, 16)
            sp.wait_ge(comb_stored, 16 * NC)
            for k in range(1, 3):
                weights(k, k)
            with sp.Fori(0, ROUNDS - 1) as r:
                for k in range(3):
                    sp.wait_ge(down_done, FREE3 + r * BODY + NC * (k + 1))
                    sp.sem_inc(env.sp_passed, 1)
                    load_matrices(sp, env, r * 3 + k + 3, k)
                    weights(r * 3 + k + 3, k)

        @block.tensor
        def _(pe):
            def gate_up(q, i, r):
                c, k = i % NC, i // NC % 3
                cs = slice(c * CH, (c + 1) * CH)
                if c == 0:
                    pe.wait_ge(wt_in[k], (r + i // BODY) * 16 + 16)
                pe.wait_ge(up_ready, q + 1)
                for bank, a, done in ((gate, 0, g_done), (up, 2, u_done)):
                    o = bank[i % 2][:, :]
                    pe.matmul(o, wt[k][:, a, :], env.xh[:, cs], start=True, stop=False)
                    pe.matmul(o, wt[k][:, a, :], env.xl[:, cs], start=False, stop=False)
                    pe.matmul(o, wt[k][:, a + 1, :], env.xh[:, cs], start=False, stop=True).then_inc(done, 1)

            def down(q, i, first, last):
                c, k = i % NC, i // NC % 3
                o = acc[c][:, :]
                skip = dict(skip_group_check=True)
                pe.wait_ge(high_ready, q + 1)
                pe.matmul(o, wt[k][:, 4, :], high[i % 3][:, :], start=first, stop=False, **skip)
                pe.matmul(o, wt[k][:, 5, :], high[i % 3][:, :], start=False, stop=False, **skip)
                pe.wait_ge(low_ready, FREE3 + q + 1)
                pe.matmul(o, wt[k][:, 4, :], low[i % 3][:, :], start=False, stop=last, **skip).then_inc(down_done, 1)

            pe.sem_inc(down_done, FREE3)
            gate_up(0, 0, 0)
            gate_up(1, 1, 0)
            for t in range(NT):
                mm = pe.transpose(acc[t // 4][0:ROWS, (t % 4) * P:(t % 4 + 1) * P], env.comb[:, t, :], env.ident[:, :])
                if t % 4 == 3:
                    mm.then_inc(comb_turned, 1)
            gate_up(2, 2, 0)
            gate_up(3, 3, 0)
            pe.wait_ge(comb_copied, NC)
            for i in range(BODY):
                gate_up(i + 4, i + 4, 0)
                down(i, i, i < NC, False)
            with pe.Fori(1, ROUNDS - 1) as r:
                for i in range(BODY):
                    gate_up(r * BODY + i + 4, i + 4, r)
                    down(r * BODY + i, i, False, False)
            for i in range(BODY):
                q = (ROUNDS - 1) * BODY + i
                if q + 4 < QN:
                    gate_up(q + 4, i + 4, ROUNDS - 1)
                down(q, i, False, i >= BODY - NC)
            for c in range(NC):
                pe.wait_ge(sum_ready, c + 1)
                if c >= 2:
                    pe.wait_ge(x_ready, c - 1)
                for t in range(4):
                    mm = pe.transpose(gate[c % 2][:, t * P:(t + 1) * P], sums[c][:, t * P:(t + 1) * P], env.ident[:, :])
                mm.then_inc(back_done, 1)

        @block.scalar
        def _(act):
            def silu(q, i):
                act.wait_ge(g_done, q + 1)
                act.activation(sil[i % 2][:, :], gate[i % 2][:, :], ACT.Silu, scale=env.unscale[:, 0:1]).then_inc(sil_ready, 1)

            def high_part(q, i):
                act.wait_ge(down_done, q + 1)
                act.wait_ge(hid_ready, ONE + q + 1)
                act.copy(high[i % 3][:, :], hid[i % 3][:, :]).then_inc(high_ready, 1)

            silu(0, 0)
            silu(1, 1)
            for c in range(NC):
                act.wait_ge(comb_turned, c + 1)
                act.copy(combT[:, c * CH:(c + 1) * CH], acc[c][0:ROWS, :]).then_inc(comb_copied, 1)
            silu(2, 2)
            high_part(0, 0)

            def body(q, i, r, last):
                if not (last and i + 3 >= BODY):
                    silu(q + 3, i + 3)
                if not (last and i + 1 >= BODY):
                    high_part(q + 1, i + 1)
            looped(act, body)
            for c in range(NC):
                act.wait_ge(down_done, FREE3 + QN - NC + c + 1)
                act.activation(sums[c][:, :], acc[c][:, :], ACT.Identity,
                               scale=env.unscale[:, 4:5]).then_inc(sum_ready, 1)

        @block.vector
        def _(dve):
            dve.tensor_copy(cb[0][:, :], env.unscale[:, 3:4].to_broadcast([P, B * S])).then_inc(cb_filled, 1)
            dve.sem_inc(up_ready, FREE_UP)
            dve.sem_inc(hid_ready, ONE)

            def times_up(q, i):
                dve.wait_ge(sil_ready, q + 1)
                dve.wait_ge(u_done, q + 1)
                dve.scalar_tensor_tensor(act_up[i % 3][:, :], up[i % 2][:, :], env.unscale[:, 1:2], sil[i % 2][:, :],
                                         ALU.mult, ALU.mult).then_inc(up_ready, 1)

            def times_weight(q, i, r):
                c, k = i % NC, i // NC % 3
                if c == 0:
                    dve.wait_ge(cb_in[k], (r + i // BODY) * 32 + 32)
                dve.wait_ge(up_ready, FREE_UP + q + 1)
                dve.wait_ge(low_ready, q + 1)
                dve.tensor_tensor(hid[i % 3][:, :], act_up[i % 3][:, :], cb[k][:, c * CH:(c + 1) * CH],
                                  ALU.mult).then_inc(hid_ready, 1)

            times_up(0, 0)
            times_up(1, 1)
            dve.wait_ge(cb_filled, 1)
            times_weight(0, 0, 0)

            def body(q, i, r, last):
                if not (last and i + 2 >= BODY):
                    dve.wait_ge(hid_ready, ONE + q)
                    times_up(q + 2, i + 2)
                if not (last and i + 1 >= BODY):
                    times_weight(q + 1, i + 1, r)
            looped(dve, body)

            for c in range(NC):
                dve.wait_ge(back_done, c + 1)
                xs = env.x[:, 4 * c:4 * c + 4, :].rearrange("p t c -> p (t c)")
                dve.tensor_tensor(xs, xs, gate[c % 2][:, :], ALU.add).then_inc(x_ready, 1)

        @block.gpsimd
        def _(pool):
            pool.sem_inc(low_ready, FREE3)

            def body(q, i, r, last):
                pool.wait_ge(high_ready, q + 1)
                pool.wait_ge(down_done, q + 1)
                pool.tensor_tensor(low[i % 3][:, :], hid[i % 3][:, :], high[i % 3][:, :], ALU.subtract).then_inc(low_ready, 1)
            looped(pool, body)


def moe(nc, env, tag):
    with ExitStack() as ctx:
        env.xh = ctx.enter_context(nc.sbuf_tensor(f"{tag}_xh", [P, B * S], F16))
        env.xl = ctx.enter_context(nc.sbuf_tensor(f"{tag}_xl", [P, B * S], F16))
        env.comb = ctx.enter_context(nc.sbuf_tensor(f"{tag}_comb", [P, NT, ROWS], F32))
        env.wt = [ctx.enter_context(nc.sbuf_tensor(f"{tag}_wt{i}", [P, 6, P], F16)) for i in range(3)]
        env.wt_in = [semaphore(nc, env, f"{tag}_wt_in{i}") for i in range(3)]
        with ExitStack() as c2:
            env.xnT = c2.enter_context(nc.sbuf_tensor(f"{tag}_xnT", [P, B * S], F32))
            route(nc, env, tag + "rt")
        experts(nc, env, tag + "ex")
    end_of_layer(nc, env)


def transformer(nc, d, out):
    env = Env()
    with ExitStack() as ctx:
        sb = lambda n, s, t: ctx.enter_context(nc.sbuf_tensor(n, s, t))
        env.semaphores = []
        env.x = sb("x_res", [P, NT, C], F32)
        env.ident = sb("ident", [P, P], F32)
        env.ident16 = sb("ident16", [P, P], BF16)
        env.masks = [sb(f"mask{i}", [P, 2 * BAND], BF16) for i in range(3)]
        env.gate = sb("gate_w", [P, E], F32)
        env.gate_bias = sb("gate_b", [P, E], F32)
        env.fresh = sb("fresh", [P, NT, E], BF16)
        env.fresh_groups = sb("fresh_g", [P, NT, GROUPS], BF16)
        env.unscale = sb("unscale", [P, 5], F32)
        env.a, env.b = Env(), Env()
        for tag, a in (("a", env.a), ("b", env.b)):
            a.tag = tag
            a.wqk = sb(tag + "_wqk", [P, 2, C], F32)
            a.bqk = sb(tag + "_bqk", [P, 2], F32)
            a.wv = sb(tag + "_wv", [P, C], F32)
            a.bv = sb(tag + "_bv", [P, C], F32)
            a.wo = sb(tag + "_wo", [P, C], F32)
            a.bo = sb(tag + "_bo", [P, C], F32)
        env.sp_passed, env.pool_passed = (ctx.enter_context(nc.semaphore(n)) for n in ("sp_passed", "pool_passed"))
        env.qs = [sb(f"qs{i}", [P, HG, S], BF16) for i in range(3)]
        env.ks = [sb(f"ks{i}", [P, HG, S], BF16) for i in range(3)]
        env.stacks = env.qs + env.ks
        env.sources = d
        env.vg = [sb(f"vg{i}", [P, TB, HG, VW], F32) for i in range(3)]
        env.stack = nc.dram_tensor("stack", [2, NG, 3, HD * HG, S], BF16).ap()
        env.stackn = env.stack.rearrange("w n s (d j) t -> w n (s d) (j t)", d=HD)
        env.wsplit = nc.dram_tensor("wsplit", [PAIRS, P, 6 * P], F16).ap()
        env.comb_rows = nc.dram_tensor("comb", [ROWS, B * S], F32).ap()
        env.comb2 = env.comb_rows.rearrange("(j e) t -> j e t", e=2)

        set_up(nc, env, d)
        attention(nc, env, env.a, "A", attend_full, first=True)
        moe(nc, env, "M1")
        attention(nc, env, env.b, "B", attend_banded)
        moe(nc, env, "M2")

        out_done = ctx.enter_context(nc.semaphore("out_done"))
        block = ctx.enter_context(nc.Block())

        @block.sync
        def _(sp):
            sp.dma_start(out.rearrange("b s c -> (b s) c").rearrange("(t p) c -> p t c", p=P),
                         env.x[:, :, :]).then_inc(out_done, 16)
            sp.wait_ge(out_done, 16)


def lay_out(np, inputs):
    get = lambda n: np.asarray(inputs["L0_" + n])
    by_width = lambda a: a.reshape(-1, G, HG, HD).transpose(0, 1, 3, 2).reshape(-1, C)
    d = {"x": get("attn_a_x")}
    for w in "ab":
        wq, wk, wv, wo = (get(f"attn_{w}_{n}") for n in ("Wq", "Wk", "Wv", "Wo"))
        if w == "a":
            wq, wk, wv, wo = wq.T, wk.T, wv.T, wo.T
        d[w + "wqk"] = np.stack([by_width(wq), by_width(wk)], 1)
        d[w + "bqk"] = np.stack([by_width(get(f"attn_{w}_bq"))[0], by_width(get(f"attn_{w}_bk"))[0]], 1)
        d[w + "wv"], d[w + "wo"] = wv, wo
        d[w + "bv"], d[w + "bo"] = get(f"attn_{w}_bv"), get(f"attn_{w}_bo")
    rows = lambda experts, shared: np.concatenate([shared, experts.reshape(-1, C)], 0)
    d["wg"] = rows(get("ffn_eg_w"), get("ffn_sg_w")).T
    d["wu"] = rows(get("ffn_eu_w"), get("ffn_su_w")).T
    down = rows(get("ffn_ed_w").transpose(0, 2, 1), get("ffn_sd_w").T)
    d["wd"] = down.reshape(PAIRS, P, C).transpose(1, 0, 2).reshape(P, -1)
    d["gate"] = get("ffn_gate_w").T
    d["gate_bias"] = get("ffn_gate_bias")
    return {n: np.ascontiguousarray(a) for n, a in d.items()}


def kernel(**inputs):
    import numpy as np
    import concourse.bacc as bacc
    from concourse.bass_utils import run_bass_kernel_spmd

    nc = bacc.Bacc("TRN2", target_bir_lowering=False, num_devices=1)
    arrays, d = {}, {}
    for name, a in lay_out(np, inputs).items():
        arrays[f"in_{name}_dram"] = a
        d[name] = nc.dram_tensor(f"in_{name}_dram", a.shape, mybir.dt.from_np(a.dtype), kind="ExternalInput").ap()
    out = nc.dram_tensor("out_0_dram", (B, S, C), F32, kind="ExternalOutput").ap()
    transformer(nc, d, out)
    r = run_bass_kernel_spmd(nc, [arrays], core_ids=[0])
    return r.results[0]["out_0_dram"]
```
